# Optimizing a Trainium2 kernel written in Bass

```python
import numpy as np
import jax
import jax.numpy as jnp

def _softmax(x, axis=-1):
    return jax.nn.softmax(x, axis=axis)

def _gelu(x):
    return jax.nn.gelu(x, approximate=True)

def _silu(x):
    return jax.nn.silu(x)

def _sigmoid(x):
    return jax.nn.sigmoid(x)

def _layernorm(x, axis=-1, eps=1e-05):
    m = jnp.mean(x, axis=axis, keepdims=True)
    v = jnp.var(x, axis=axis, keepdims=True)
    return (x - m) / jnp.sqrt(v + eps)

def _scatter_add(tgt, idx, src, axis=0):
    return tgt.at[idx].add(src)

def _segment_sum(src, seg, n):
    return jax.ops.segment_sum(src, seg, n)
kernel_name = 'mk_gps_d1_gnn_r8_ec9a5a'

def setup_inputs(seed: int=0):
    np.random.seed(seed)
    _w = jnp.asarray

    def _rec_inputs():
        import jax
        import jax.numpy as jnp
        _gk = jax.random.key(seed)
        x = -8.776e-05 + 1 * jax.random.normal(jax.random.fold_in(_gk, 1), (6250, 256), jnp.float32)
        src = jax.random.randint(jax.random.fold_in(_gk, 2), (200000,), 0, 6250, jnp.int32)
        dst = jnp.minimum((6250 * jax.random.uniform(jax.random.fold_in(_gk, 3), (200000,)) ** 2.0).astype(jnp.int32), 49999)
        _o = jnp.argsort(dst, stable=True)
        src = src[_o]
        dst = dst[_o]
        edge_type_32 = jax.random.randint(jax.random.fold_in(_gk, 12), (200000,), 0, 32, jnp.int32)
        edge_weight1 = jax.random.uniform(jax.random.fold_in(_gk, 13), (200000, 1), jnp.float32, 0.0, 0.999998)
        return (x, src, dst, edge_type_32, edge_weight1)
    x, src, dst, edge_type_32, edge_weight1 = _rec_inputs()

    def _L0_gnn_setup():
        import jax, jax.numpy as jnp
        import numpy as np
        N_NODES = 2500
        N_EDGES = 40000
        IN_DIM = 256
        OUT_DIM = 256
        NUM_RELS = 32
        NUM_BASES = 8
        key = jax.random.key(seed)
        k1, k2, k3, k4, k5, k6, k7 = jax.random.split(key, 7)
        h = jax.random.normal(k1, (N_NODES, IN_DIM), dtype=jnp.float32)
        src = jax.random.randint(k2, (N_EDGES,), 0, N_NODES, dtype=jnp.int32)
        dst = jax.random.randint(k3, (N_EDGES,), 0, N_NODES, dtype=jnp.int32)
        rel_type = jax.random.randint(k4, (N_EDGES,), 0, NUM_RELS, dtype=jnp.int32)
        norm = jax.random.uniform(k5, (N_EDGES, 1), dtype=jnp.float32)
        scale_w = np.sqrt(2.0) * np.sqrt(6.0 / (IN_DIM + OUT_DIM))
        bases = jax.random.uniform(k6, (NUM_BASES, IN_DIM, OUT_DIM), dtype=jnp.float32, minval=-scale_w, maxval=scale_w)
        scale_c = np.sqrt(2.0) * np.sqrt(6.0 / (NUM_RELS + NUM_BASES))
        w_comp = jax.random.uniform(k7, (NUM_RELS, NUM_BASES), dtype=jnp.float32, minval=-scale_c, maxval=scale_c)
        return {'h': h, 'src': src, 'dst': dst, 'rel_type': rel_type, 'norm': norm, 'bases': bases, 'w_comp': w_comp}
    _L0_gnn_all = _L0_gnn_setup()
    _L0_gnn_in = {k: v for k, v in _L0_gnn_all.items() if k in ('bases', 'w_comp')}
    del _L0_gnn_all

    def _L0_mix_setup():
        import jax, jax.numpy as jnp
        import numpy as np
        NHEAD = 8
        ATT_EPS = 1e-06
        LN_EPS = 1e-05

        def _layernorm(x, g, b):
            mu = jnp.mean(x, axis=-1, keepdims=True)
            var = jnp.mean(jnp.square(x - mu), axis=-1, keepdims=True)
            return (x - mu) * jax.lax.rsqrt(var + LN_EPS) * g + b
        key = jax.random.key(seed)
        ks = jax.random.split(key, 7)
        N, L, C = (4, 2048, 256)
        s = 1.0 / np.sqrt(C)
        return {'x': jax.random.normal(ks[0], (N, L, C), jnp.float32), 'Wq': jax.random.normal(ks[1], (C, C), jnp.float32) * s, 'Wk': jax.random.normal(ks[2], (C, C), jnp.float32) * s, 'Wv': jax.random.normal(ks[3], (C, C), jnp.float32) * s, 'Wm': jax.random.normal(ks[4], (C, C), jnp.float32) * s, 'W1': jax.random.normal(ks[5], (2 * C, 2 * C), jnp.float32) * (1.0 / np.sqrt(2 * C)), 'W2': jax.random.normal(ks[6], (2 * C, C), jnp.float32) * (1.0 / np.sqrt(2 * C)), 'g1': jnp.ones((C,), jnp.float32), 'b1': jnp.zeros((C,), jnp.float32), 'g2': jnp.ones((C,), jnp.float32), 'b2': jnp.zeros((C,), jnp.float32)}
    _L0_mix_all = _L0_mix_setup()
    _L0_mix_in = {k: v for k, v in _L0_mix_all.items() if k in ('Wq', 'Wk', 'Wv', 'Wm', 'W1', 'W2', 'g1', 'b1', 'g2', 'b2')}
    del _L0_mix_all

    def _L0_ffn_setup():
        import jax, jax.numpy as jnp
        import numpy as np
        BN_EPS = 0.001

        def _bn(h, g, b, m, v):
            return g * (h - m) * jax.lax.rsqrt(v + BN_EPS) + b
        key = jax.random.key(seed)
        ks = jax.random.split(key, 8)
        B, F, Df = (256, 64, 256)
        E, H, D = (8, 256, 256)
        s1 = 1.0 / np.sqrt(Df)
        s2 = 1.0 / np.sqrt(H)
        return {'x': jax.random.normal(ks[0], (B, F, Df), jnp.float32), 'Wr': jax.random.normal(ks[1], (Df, E), jnp.float32) * s1, 'br': jnp.zeros((E,), jnp.float32), 'W1': jax.random.normal(ks[2], (E, Df, H), jnp.float32) * s1, 'b1': jnp.zeros((E, H), jnp.float32), 'g1': jnp.ones((E, H), jnp.float32), 'be1': jnp.zeros((E, H), jnp.float32), 'm1': jnp.zeros((E, H), jnp.float32), 'v1': jnp.ones((E, H), jnp.float32), 'W2': jax.random.normal(ks[3], (E, H, H), jnp.float32) * s2, 'b2': jnp.zeros((E, H), jnp.float32), 'g2': jnp.ones((E, H), jnp.float32), 'be2': jnp.zeros((E, H), jnp.float32), 'm2': jnp.zeros((E, H), jnp.float32), 'v2': jnp.ones((E, H), jnp.float32), 'Wo': jax.random.normal(ks[4], (E, H, D), jnp.float32) * s2, 'bo': jnp.zeros((E, D), jnp.float32)}
    _L0_ffn_all = _L0_ffn_setup()
    _L0_ffn_in = {k: v for k, v in _L0_ffn_all.items() if k in ('Wr', 'br', 'W1', 'b1', 'g1', 'be1', 'm1', 'v1', 'W2', 'b2', 'g2', 'be2', 'm2', 'v2', 'Wo', 'bo')}
    del _L0_ffn_all
    return {'x': x, 'src': src, 'dst': dst, 'edge_type_32': edge_type_32, 'edge_weight1': edge_weight1, 'L0_gnn_bases': _L0_gnn_in['bases'], 'L0_gnn_w_comp': _L0_gnn_in['w_comp'], 'L0_mix_Wq': _L0_mix_in['Wq'], 'L0_mix_Wk': _L0_mix_in['Wk'], 'L0_mix_Wv': _L0_mix_in['Wv'], 'L0_mix_Wm': _L0_mix_in['Wm'], 'L0_mix_W1': _L0_mix_in['W1'], 'L0_mix_W2': _L0_mix_in['W2'], 'L0_mix_g1': _L0_mix_in['g1'], 'L0_mix_b1': _L0_mix_in['b1'], 'L0_mix_g2': _L0_mix_in['g2'], 'L0_mix_b2': _L0_mix_in['b2'], 'L0_ffn_Wr': _L0_ffn_in['Wr'], 'L0_ffn_br': _L0_ffn_in['br'], 'L0_ffn_W1': _L0_ffn_in['W1'], 'L0_ffn_b1': _L0_ffn_in['b1'], 'L0_ffn_g1': _L0_ffn_in['g1'], 'L0_ffn_be1': _L0_ffn_in['be1'], 'L0_ffn_m1': _L0_ffn_in['m1'], 'L0_ffn_v1': _L0_ffn_in['v1'], 'L0_ffn_W2': _L0_ffn_in['W2'], 'L0_ffn_b2': _L0_ffn_in['b2'], 'L0_ffn_g2': _L0_ffn_in['g2'], 'L0_ffn_be2': _L0_ffn_in['be2'], 'L0_ffn_m2': _L0_ffn_in['m2'], 'L0_ffn_v2': _L0_ffn_in['v2'], 'L0_ffn_Wo': _L0_ffn_in['Wo'], 'L0_ffn_bo': _L0_ffn_in['bo']}

def reference(x, src, dst, edge_type_32, edge_weight1, L0_gnn_bases, L0_gnn_w_comp, L0_mix_Wq, L0_mix_Wk, L0_mix_Wv, L0_mix_Wm, L0_mix_W1, L0_mix_W2, L0_mix_g1, L0_mix_b1, L0_mix_g2, L0_mix_b2, L0_ffn_Wr, L0_ffn_br, L0_ffn_W1, L0_ffn_b1, L0_ffn_g1, L0_ffn_be1, L0_ffn_m1, L0_ffn_v1, L0_ffn_W2, L0_ffn_b2, L0_ffn_g2, L0_ffn_be2, L0_ffn_m2, L0_ffn_v2, L0_ffn_Wo, L0_ffn_bo):
    import jax
    import jax.numpy as jnp

    def _L0_gnn_ref(h, src, dst, rel_type, norm, bases, w_comp):
        import jax, jax.numpy as jnp
        import numpy as np
        N_NODES = 2500
        N_EDGES = 40000
        IN_DIM = 256
        OUT_DIM = 256
        NUM_RELS = 32
        NUM_BASES = 8
        weight = jnp.einsum('rb,bio->rio', w_comp, bases)
        xw = jnp.einsum('ni,rio->nro', h, weight)
        msg = xw[src, rel_type] * norm
        out = jax.ops.segment_sum(msg, dst, num_segments=h.shape[0])
        return jax.nn.relu(out)

    def _L0_mix_ref(x, Wq, Wk, Wv, Wm, W1, W2, g1, b1, g2, b2):
        import jax, jax.numpy as jnp
        import numpy as np
        NHEAD = 8
        ATT_EPS = 1e-06
        LN_EPS = 1e-05

        def _layernorm(x, g, b):
            mu = jnp.mean(x, axis=-1, keepdims=True)
            var = jnp.mean(jnp.square(x - mu), axis=-1, keepdims=True)
            return (x - mu) * jax.lax.rsqrt(var + LN_EPS) * g + b
        N, L, C = x.shape
        H = NHEAD
        D = C // H
        q = (x @ Wq).reshape(N, L, H, D)
        k = (x @ Wk).reshape(N, L, H, D)
        v = (x @ Wv).reshape(N, L, H, D)
        Q = jax.nn.elu(q) + 1.0
        K = jax.nn.elu(k) + 1.0
        v = v / L
        KV = jnp.einsum('nshd,nshv->nhdv', K, v)
        Z = 1.0 / (jnp.einsum('nlhd,nhd->nlh', Q, K.sum(axis=1)) + ATT_EPS)
        msg = jnp.einsum('nlhd,nhdv,nlh->nlhv', Q, KV, Z) * L
        msg = msg.reshape(N, L, C) @ Wm
        msg = _layernorm(msg, g1, b1)
        h = jnp.concatenate([x, msg], axis=-1) @ W1
        h = jax.nn.relu(h) @ W2
        msg = _layernorm(h, g2, b2)
        return x + msg

    def _L0_ffn_ref(x, Wr, br, W1, b1, g1, be1, m1, v1, W2, b2, g2, be2, m2, v2, Wo, bo):
        import jax, jax.numpy as jnp
        import numpy as np
        BN_EPS = 0.001

        def _bn(h, g, b, m, v):
            return g * (h - m) * jax.lax.rsqrt(v + BN_EPS) + b
        feat = jnp.mean(x, axis=0)
        w = jax.nn.softmax(feat @ Wr + br, axis=-1)
        h = jnp.einsum('bfd,edh->bfeh', x, W1) + b1
        h = jax.nn.relu(_bn(h, g1, be1, m1, v1))
        h = jnp.einsum('bfeh,ehk->bfek', h, W2) + b2
        h = jax.nn.relu(_bn(h, g2, be2, m2, v2))
        y = jnp.einsum('bfeh,ehd->bfed', h, Wo) + bo
        return jnp.einsum('bfed,fe->bfd', y, w)
    xn = _layernorm(x, axis=-1)
    x = x + _L0_gnn_ref(xn, src, dst, edge_type_32, edge_weight1, L0_gnn_bases, L0_gnn_w_comp) + _L0_mix_ref(xn[None], L0_mix_Wq, L0_mix_Wk, L0_mix_Wv, L0_mix_Wm, L0_mix_W1, L0_mix_W2, L0_mix_g1, L0_mix_b1, L0_mix_g2, L0_mix_b2)[0]
    x = x + _L0_ffn_ref(_layernorm(x, axis=-1)[None], L0_ffn_Wr, L0_ffn_br, L0_ffn_W1, L0_ffn_b1, L0_ffn_g1, L0_ffn_be1, L0_ffn_m1, L0_ffn_v1, L0_ffn_W2, L0_ffn_b2, L0_ffn_g2, L0_ffn_be2, L0_ffn_m2, L0_ffn_v2, L0_ffn_Wo, L0_ffn_bo)[0]
    return x

_drawn_inputs = setup_inputs


def setup_inputs(seed=0):
    import zlib

    import numpy as np

    out = dict(_drawn_inputs(seed))
    spreads = {'L0_mix_g1': (1.0, 0.2),
     'L0_mix_b1': (0.0, 0.44),
     'L0_mix_g2': (1.0, 0.2),
     'L0_mix_b2': (0.0, 0.302),
     'L0_ffn_br': (0.0, 0.8),
     'L0_ffn_b1': (0.0, 0.8),
     'L0_ffn_g1': (1.0, 0.6),
     'L0_ffn_be1': (0.0, 0.8),
     'L0_ffn_m1': (0.0, 0.8),
     'L0_ffn_v1': (1.0, 0.6),
     'L0_ffn_b2': (0.0, 0.8),
     'L0_ffn_g2': (1.0, 0.6),
     'L0_ffn_be2': (0.0, 0.8),
     'L0_ffn_m2': (0.0, 0.8),
     'L0_ffn_v2': (1.0, 0.6),
     'L0_ffn_bo': (0.0, 0.618)}
    factors = {}
    for name, (base, spread) in spreads.items():
        noise = np.random.default_rng([zlib.crc32(name.encode()), seed]).standard_normal(out[name].shape)
        drawn = base * np.exp(spread * noise) if base else spread * noise
        out[name] = jnp.asarray(drawn.astype(out[name].dtype))
    for name, factor in factors.items():
        out[name] = (out[name] * factor).astype(out[name].dtype)
    return out
```

```python
import concourse.bass as bass
from concourse import mybir
from contextlib import ExitStack

F32 = mybir.dt.float32
BF16 = mybir.dt.bfloat16
I32 = mybir.dt.int32
ALU = mybir.AluOpType
ACT = mybir.ActivationFunctionType
AX = mybir.AxisListType

P = 128
NODES, C = 6250, 256
EDGES = 200000
RELS, BASES = 32, 8
HEADS = 8
HD = C // HEADS
EXPERTS = 8
KH = C // P
TILES = -(-NODES // P)
LAST = NODES - (TILES - 1) * P
CHUNKS = -(-EDGES // P)
FULLC = EDGES // P
TAILE = EDGES - FULLC * P
CB = -(-CHUNKS // P)
CREST = CHUNKS - (CB - 1) * P

GN = P // BASES
GROUPS = -(-NODES // GN)
STEPS = CHUNKS + GROUPS - 1
UN = 20
ITERS = 2 * TILES
RING = 10
BATCH = 5
NB = UN // BATCH
SLOTS = 4
SB = 16
SPAD = SB * P
GPAD = 400
assert ITERS * UN >= STEPS and (ITERS + 2) * UN <= SPAD and ITERS * UN - CHUNKS < GPAD
assert UN % RING == 0 and UN % SLOTS == 0 and RING == 2 * BATCH

FAR = 8191
FAR_GROUP = FAR // GN
LN_EPS, ATT_EPS, BN_EPS = 1e-5, 1e-6, 1e-3
RSQRT_SEED = 0x5F3759DF
NEWTON = 3
NR1 = 2 + 3 * NEWTON
NRW = 2 + 4 * NEWTON

LG = 8
LT = (TILES - 1) // LG // 2
SUP = 4
SUPERS = (TILES - 1) // SUP
SORTK = 392


def gps_layer(nc, x, src, dst, etype, eweight, bases, w_comp, Wq, Wk, Wv, Wm, W1, W2, g1, b1, g2, b2,
              Wr, br, fW1, fb1, fg1, fbe1, fm1, fv1, fW2, fb2, fg2, fbe2, fm2, fv2, Wo, bo, out):
    ctx = ExitStack()
    with ctx:
        sems = {}

        def sem(name):
            if name not in sems:
                sems[name] = ctx.enter_context(nc.semaphore(name))
            return sems[name]

        def sb(name, shape, dt=F32):
            return ctx.enter_context(nc.sbuf_tensor(name, shape, dt))

        rec = nc.dram_tensor("edge_records", [CHUNKS, 4 * P], I32).ap()
        srt = nc.dram_tensor("sorted_edges", [CHUNKS * P, 4], I32).ap()
        cflat = nc.dram_tensor("step_chunks", [SPAD, 1], F32).ap()
        relS = nc.dram_tensor("step_types", [SPAD, P], F32).ap()
        xnD = nc.dram_tensor("normed_nodes", [(TILES + 1) * P, C], F32).ap()
        baseD = nc.dram_tensor("mix_result", [TILES * P, C], F32).ap()
        aggD = nc.dram_tensor("aggregates", [GPAD, P, C], F32).ap()

        ident = sb("ident", [P, P])
        ones = sb("ones", [P, P])
        iota16 = sb("iota16", [P, GN])
        relcol = sb("relcol", [P, 1])
        chunk_no = sb("chunk_no", [P, CB])
        step_no = sb("step_no", [P, SB])
        wblk = sb("wblk", [P, 4 * BASES])
        kvmask = sb("kvmask", [P, P])
        headmask = sb("headmask", [P, 4])
        rowmask = sb("rowmask", [P, TILES])
        wq_s = sb("wq_s", [P, KH, C])
        wkv_s = sb("wkv_s", [P, KH, 2 * C])
        wm_s = sb("wm_s", [P, KH, C])
        w1_s = sb("w1_s", [P, 4, 2 * C])
        w2_s = sb("w2_s", [P, 4, C])
        lnw = sb("lnw", [P, 4, C])
        wr_s = sb("wr_s", [P, KH, EXPERTS])
        br_s = sb("br_s", [P, EXPERTS])
        bo_s = sb("bo_s", [EXPERTS, C])
        bases_s = sb("bases_s", [P, BASES, KH, C])
        ffw = sb("ffw", [P, 3 * EXPERTS * KH * C])
        f1_s, f2_s, fo_s = (ffw[:, n * EXPERTS * KH * C:(n + 1) * EXPERTS * KH * C].rearrange(
            "p (e k n) -> p e k n", e=EXPERTS, k=KH) for n in range(3))
        bnc = sb("bnc", [P, 4, 2 * EXPERTS])

        def carver(name, words):
            t = sb(name, [P, words])
            place = [0]

            def carve(n, at=None):
                a = place[0] if at is None else at
                place[0] = max(place[0], a + n)
                assert place[0] <= words, (name, place[0])
                return t[:, a:a + n]
            return carve

        ARENA = 20480
        carve = carver("arena", ARENA)
        ring = carve(RING * C).rearrange("p (r n) -> p r n", r=RING)
        acc = carve(RING * C).rearrange("p (r n) -> p r n", r=RING)
        selm = carve(2 * BATCH * P).rearrange("p (u s n b) -> p u s n b", u=2, s=BATCH, b=BASES)
        relb = carve(BATCH * P).rearrange("p (j e) -> p j e", j=BATCH)
        relhot = carve(BATCH * P).rearrange("p (j e) -> p j e", j=BATCH)
        table = carve(3 * SPAD).rearrange("p (f s) -> p f s", f=3)
        keep = carve(SPAD)
        rowsI = carve(SPAD).bitcast(I32)
        grow = rowsI[0:1, :]
        hot = carve(UN * GN).rearrange("p (s n) -> p s n", s=UN)
        coef = carve(UN * BASES).rearrange("p (s b) -> p s b", s=UN)
        keepc = carve(UN)
        idxc = carve(UN).bitcast(I32)
        irec = carve(4 * 4 * P, 0).bitcast(I32).rearrange("p (u n) -> p u n", u=4)
        ifld = carve(4 * 3 * P, RING * C).rearrange("p (u f n) -> p u f n", u=4, f=3)
        junk = carve(CB * P // 2, RING * C + 4 * 3 * P).bitcast(BF16)
        crow = carve(SPAD + 1, 2 * RING * C)
        chk_a = carve(EDGES // 125, 0)[0:125, :].bitcast(I32)
        chk_b = carve(EDGES // 125, RING * C)[0:125, :].bitcast(I32)
        chk_c = carve(EDGES // 125, 2 * RING * C + 2 * BATCH * P + 2 * BATCH * P)[0:125, :]
        CHKP, CHKN = 125, EDGES // 125

        def tiled(at):
            return carve(SUP * C, at).rearrange("p (j n) -> p j n", j=SUP)

        at_in = carve(SUP * 8 * C, 0).rearrange("p (j h g n) -> p j h g n", j=SUP, h=KH, g=8)
        base_in, x_in, xr, x1, x1n, oacc = (tiled((8 + n) * SUP * C) for n in range(6))
        x1t, h1, h2 = (carve(KH * SUP * P, (14 + n) * SUP * C).rearrange("p (k n) -> p k n", k=KH) for n in range(3))
        rest = 17 * SUP * C
        lg, ex, rw = (carve(SUP * EXPERTS, rest + n * SUP * EXPERTS) for n in range(3))
        rmx, rsm, rin = (carve(SUP, rest + 3 * SUP * EXPERTS + n * SUP) for n in range(3))
        bst = carve(SUP * 6, rest + 4 * SUP * EXPERTS).rearrange("p (j n) -> p j n", j=SUP)
        bmv = carve(SUP * 2, rest + 5 * SUP * EXPERTS).rearrange("p (j n) -> p j n", j=SUP)
        wt = carve(SUP * P, rest + 6 * SUP * EXPERTS)[0:EXPERTS, :]

        lns = sb("lns", [P, LT, 6])
        lnmv = sb("lnmv", [P, LT, 2])
        nrw = sb("nrw", [P, 4, P])
        nri = sb("nri", [P, P], I32)
        cstep = sb("cstep", [P, SB])
        cint = sb("cint", [P, SB], I32)
        gbase = sb("gbase", [P, 2, SB])
        colc = sb("colc", [P, 4], I32)
        colg = sb("colg", [P, 4])
        fdst = sb("fdst", [P, CB], I32)
        fgrp = sb("fgrp", [P, CB], I32)
        tcol = sb("tcol", [P, CB])
        diag = sb("diag", [P, 2, P])
        PADE = P - TAILE
        padc = sb("padc", [1, 4 * PADE], I32)
        zrow = sb("zrow", [P, KH * (P + 1)])
        flag = sb("flag", [1, 1], I32)
        flagf = sb("flagf", [P, 1])
        mix = carver("mixbuf", 22 * C)
        xt, xr2, ek, rk, ksb, msb = (mix(C) for _ in range(6))
        xnt, mst, qt = (mix(C).rearrange("p (k n) -> p k n", k=KH) for _ in range(3))
        cat = mix(2 * C).rearrange("p (k n) -> p k n", k=4)
        ht = mix(2 * C).rearrange("p (k n) -> p k n", k=4)
        mn = mix(3 * C).rearrange("p (k n) -> p k n", k=3)
        mo = mix(4 * C).rearrange("p (k n) -> p k n", k=4)
        vx = sb("vx", [P, KH, P + 1])
        kvb = sb("kvb", [P, KH, P + 4])
        zt = sb("zt", [P, HEADS])
        zi = sb("zi", [P, HEADS])
        lst = sb("lst", [P, 6])
        lmv = sb("lmv", [P, 2])
        lnx = mix(2 * LT * C, 0).rearrange("p (h t n) -> p h t n", h=2, t=LT)
        bnrow = mix(10 * P, 2 * LT * C)[0:2 * EXPERTS, :].rearrange("p (v n) -> p v n", v=10)
        bnt = mix(4 * P, 2 * LT * C + 10 * P)[0:2 * EXPERTS, :].rearrange("p (v n) -> p v n", v=4)
        bnd = mix(P, 2 * LT * C + 14 * P)[0:2 * EXPERTS, :]

        PS = ctx.enter_context(nc.psum_tensor("PS", [P, 8 * 512], F32))

        def bank(n, a=0, b=512):
            return PS[:, n * 512 + a:n * 512 + b]

        so = [0]

        def carve_s(words):
            at = so[0]
            so[0] += words
            assert so[0] <= 3 * EXPERTS * KH * C
            return ffw[:, at:at + words]

        s_dst = carve_s(CHUNKS).bitcast(I32)
        s_oth = carve_s(3 * CHUNKS).rearrange("p (f n) -> p f n", f=3).bitcast(I32)
        s_key = carve_s(CHUNKS)
        s_rank = carve_s(CHUNKS)
        s_iota = carve_s(SORTK)
        s_run = carve_s(SORTK)
        s_start = carve_s(SORTK)
        s_tmp = carve_s(SORTK)
        s_one = carve_s(SORTK // 2).bitcast(BF16)
        s_low = carve_s(P // 2).bitcast(BF16)
        s_all = carve_s(P // 2).bitcast(BF16)
        s_col = carve_s(2)
        s_idx = carve_s(1).bitcast(I32)
        s_rec = carve_s(4).bitcast(I32)
        s_blk = bases_s[:, :, :, :].rearrange("p a b n -> p (a b n)")[:, 0:8 * P].bitcast(I32).rearrange(
            "p (h n) -> p h n", h=2)

        def wait_apart(eng, name, value):
            eng.wait_ge(sem(name), value)
            eng.sem_inc(sem("passed"), 1)

        LEAD, DLEAD = 1, 16
        LED = {
            "pe": ("m1_kv", "m1_acc", "m2_w1", "m2_wm", "m2_w2", "m2_msg", "m2_tm", "m2_tn", "coef_mm", "fld_tp",
                   "f_l1", "f_l2", "f_l3", "b_mm", "b_tp"),
            "dve": ("m1_k", "m2_qt", "m2_base", "m2_2n", "coef_ready", "sel_ready", "b_x", "b_r", "o_upd"),
            "act": ("m1_xt", "m1_v", "m2_nt", "m2_h", "table_cp", "b_xt", "f_h1", "f_h2"),
        }

        def start_ahead(eng, who):
            for name in LED[who]:
                eng.sem_inc(sem(name), LEAD)

        LED_DMA = ["ln_st0", "ln_st1", "base_out", "out_st"] + [f"rels_out{u}" for u in range(4)] + \
                  [f"flush{r}" for r in range(RING)]
        lead_s = sb("lead_s", [1, 4 * (len(LED_DMA) + 1)])

        def dma_ahead(eng, name, n):
            eng.dma_start(lead_s[:, 4 * n:4 * n + 4], x[0:1, 0:4]).then_inc(sem(name), DLEAD)

        class Chain:

            def __init__(self, eng, name):
                self.eng, self.name, self.n = eng, name, 0

            def __call__(self, ins, apart=False):
                self.n = self.n + 1
                ins.then_inc(sem(self.name), 1)
                if apart:
                    wait_apart(self.eng, self.name, self.n)
                else:
                    self.eng.wait_ge(sem(self.name), self.n)

        block = ctx.enter_context(nc.Block())
        def rows(ap, k):
            return ap.rearrange("(k p) n -> p k n", p=P)

        @block.sync
        def _(sp):
            for n, name in enumerate(LED_DMA):
                dma_ahead(sp, name, n)
            sp.dma_start(chk_a, dst.rearrange("(p n) -> p n", p=CHKP)).then_inc(sem("chk_in"), 16)
            sp.wait_ge(sem("dve_const"), 2)
            sp.dma_start(chk_b[0:CHKP - 1, :],
                         dst[1:1 + (CHKP - 1) * CHKN].rearrange("(p n) -> p n", n=CHKN)).then_inc(sem("chk_in"), 16)
            sp.dma_start(chk_b[CHKP - 1:CHKP, 0:CHKN - 1],
                         dst[1 + (CHKP - 1) * CHKN:EDGES].rearrange("(p n) -> p n", p=1)).then_inc(sem("chk_in"), 16)
            fields = [src, dst, etype, eweight.rearrange("e a -> (e a)").bitcast(I32)]
            for f, v in enumerate(fields):
                sp.dma_start(rec[0:FULLC, f * P:(f + 1) * P],
                             v[0:FULLC * P].rearrange("(c e) -> c e", e=P)).then_inc(sem("rec_in"), 16)
                sp.dma_start(rec[FULLC:CHUNKS, f * P:f * P + TAILE],
                             v[FULLC * P:EDGES].rearrange("(a e) -> a e", a=1)).then_inc(sem("rec_in"), 16)
            sp.wait_ge(sem("dve_const"), 5)
            sp.dma_start(rec[FULLC:CHUNKS, :].rearrange("a (f e) -> a f e", f=4)[:, :, TAILE:P],
                         padc[:, :].rearrange("a (f e) -> a f e", f=4)).then_inc(sem("rec_in"), 16)
            sp.wait_ge(sem("dve_const"), 6)
            sp.dma_start(xnD[TILES * P:(TILES + 1) * P, :], zrow[:, 0:C]).then_inc(sem("xn_out"), 16)
            with sp.Fori(0, LG) as i:
                for h in range(2):
                    at = i * (2 * LT * P) + h * LT * P
                    sp.wait_ge(sem(f"ln_st{h}"), DLEAD + 16 * i)
                    sp.dma_start(lnx[:, h, :, :], x[bass.ds(at, LT * P), :].rearrange("(t p) n -> p t n", p=P)
                                 ).then_inc(sem(f"ln_ld{h}"), 16)
            sp.wait_ge(sem("ln_st0"), DLEAD + 16 * LG)
            sp.wait_ge(sem("ln_zero"), 1)
            sp.dma_start(lnx[0:LAST, 0, 0, :], x[(TILES - 1) * P:NODES, :]).then_inc(sem("ln_ld0"), 16)

            sp.wait_ge(sem("flag_ready"), 1)
            unsorted = sp.value_load(flag[0:1, 0:1], min_val=0, max_val=1)
            with sp.If(unsorted > 0):
                sp.wait_ge(sem("s_fill"), 2)
                sp.wait_ge(sem("rec_in"), 16 * 9)
                lane = (P - 1) * CHUNKS
                for n, (t, v) in enumerate(((s_dst, dst), (s_oth[:, 0, :], src), (s_oth[:, 1, :], etype),
                                            (s_oth[:, 2, :], fields[3]))):
                    sp.dma_start(t[0:P - 1, :], v[0:lane].rearrange("(p n) -> p n", n=CHUNKS)
                                 ).then_inc(sem("s_in"), 16)
                    sp.dma_start(t[P - 1:P, 0:EDGES - lane], v[lane:EDGES].rearrange("(a n) -> a n", a=1)
                                 ).then_inc(sem("s_in"), 16)
                sp.wait_ge(sem("s_scat"), DLEAD + 16 * CHUNKS)
                for j in range(CB):
                    n = P if j < CB - 1 else CREST
                    if j:
                        sp.wait_ge(sem("s_rout"), 16 * j)
                    sp.dma_start(s_blk[0:n, 0, :], srt[j * P * P:j * P * P + n * P, :].rearrange(
                        "(c e) f -> c (e f)", e=P)).then_inc(sem("s_rin"), 16)
                    sp.wait_ge(sem("s_turn"), 2 * j + 2)
                    sp.dma_start(rec[j * P:j * P + n, :], s_blk[0:n, 1, :]).then_inc(sem("s_rout"), 16)
                sp.wait_ge(sem("s_rout"), 16 * CB)
            sp.wait_ge(sem("rec_in"), 16 * 9)
            sp.sem_inc(sem("rec_ready"), 1)

            with nc.allow_non_contiguous_dma(reason="one word per chunk"):
                sp.wait_ge(sem("dve_const"), 7)
                sp.dma_start(fdst[:, 0:CB - 1], rec[0:(CB - 1) * P, P:P + 1].rearrange(
                    "(j p) a -> p (j a)", p=P), allow_slow_non_contiguous=True).then_inc(sem("fdst_in"), 16)
                sp.dma_start(fdst[0:CREST, CB - 1:CB], rec[(CB - 1) * P:CHUNKS, P:P + 1]
                             ).then_inc(sem("fdst_in"), 16)
                sp.wait_ge(sem("cstep_ready"), SB)
                sp.dma_start(cflat.rearrange("(j p) a -> p (j a)", p=P), cstep[:, :],
                             allow_slow_non_contiguous=True).then_inc(sem("cflat_out"), 16)
            sp.wait_ge(sem("cflat_out"), 16)
            sp.dma_start(crow[:, 1:SPAD + 1], cflat.rearrange("s a -> a s").to_broadcast([P, SPAD])
                         ).then_inc(sem("crow_in"), 16)
            with sp.Fori(0, SB // 4) as i:
                for u in range(4):
                    sp.wait_ge(sem("fld_type"), 4 * i + u + 1)
                    sp.dma_start(relS[bass.ds((4 * i + u) * P, P), :], ifld[:, u, 2, :]
                                 ).then_inc(sem(f"rels_out{u}"), 16)
            for u in range(4):
                sp.wait_ge(sem(f"rels_out{u}"), DLEAD + 16 * (SB // 4))

            def load_types(it):
                v = relS.rearrange("(j q) e -> q j e", q=4)
                for q in range(4):
                    s = v[q:q + 1, bass.ds(it * BATCH, BATCH), :]
                    sp.dma_start(relb[32 * q:32 * q + 32, :, :], s.to_broadcast([32, BATCH, P])
                                 ).then_inc(sem("types_in"), 16)

            load_types(0)
            sp.wait_ge(sem("relhot_ready"), 1)
            load_types(1)
            sp.wait_ge(sem("xn_out"), 16)
            sp.wait_ge(sem("ln_st0"), DLEAD + 16 * (LG + 1))
            sp.wait_ge(sem("ln_st1"), DLEAD + 16 * LG)
            sp.sem_inc(sem("xn_ready"), 1)
            sp.dma_start(xt[:, :], xnD[0:P, :]).then_inc(sem("xt_in"), 16)
            sp.wait_ge(sem("tables_ready"), 2)

            gregs = [sp.alloc_register(f"group{k}") for k in range(UN + 1)]

            def steps(it, extra):
                sp.load(gregs, grow[:, bass.ds(it * UN, UN + 1)])
                g = [sp.snap(r, min_val=0, max_val=GPAD - 1) for r in gregs]
                for k in range(UN):
                    s = it * UN + k
                    if k in extra:
                        extra[k]()
                    sp.wait_ge(sem("acc_done"), s + 1 + SLOTS)
                    sp.dma_start(aggD[bass.ds(g[k], 1), :, :].rearrange("a p n -> p (a n)"), acc[:, k % RING, :],
                                 cond=(g[k + 1] > g[k])).then_inc(sem(f"flush{k % RING}"), 16)

            def next_types(it):
                sp.wait_ge(sem("relhot_ready"), it + 2)
                load_types(it + 2)

            with sp.Fori(0, TILES) as i:
                def next_x():
                    sp.wait_ge(sem("m1_tp"), i + 1)
                    sp.dma_start(xt[:, :], xnD[bass.ds((i + 1) * P, P), :]).then_inc(sem("xt_in"), 16)
                steps(i, {5: next_x, 12: lambda: next_types(i)})
            sp.wait_ge(sem("m1_tp"), TILES)
            sp.dma_start(xt[:, :], xnD[0:P, :]).then_inc(sem("xt_in"), 16)
            with sp.Fori(0, TILES) as i:
                def next_x2():
                    sp.wait_ge(sem("m2_tp"), i + 1)
                    sp.dma_start(xt[:, :], xnD[bass.ds((i + 1) * P, P), :]).then_inc(sem("xt_in"), 16)
                    sp.wait_ge(sem("m2_base"), LEAD + i)
                    sp.dma_start(xr2[:, :], xnD[bass.ds(i * P, P), :]).then_inc(sem("xr2_in"), 16)
                steps(i + TILES, {5: next_x2, 12: lambda: next_types(i + TILES)})
            sp.wait_ge(sem("xt_in"), 32 * (TILES + 1))
            sp.wait_ge(sem("types_in"), 64 * (ITERS + 2))
            for r in range(RING):
                sp.wait_ge(sem(f"flush{r}"), DLEAD + 16 * ITERS * UN // RING)
            sp.wait_ge(sem("base_out"), DLEAD + 16 * TILES)
            sp.wait_ge(sem("main_over"), 4)

            def load_super(i, tiles, n):
                for j in range(tiles):
                    t = i * SUP + j
                    sp.wait_ge(sem("b_mm"), LEAD + i * SUP)
                    for h in range(KH):
                        sp.dma_start(at_in[:, j, h, :, :], aggD[bass.ds(t * 8, 8), :, h * P:(h + 1) * P].rearrange(
                            "g p n -> p g n")).then_inc(sem(f"at_in{j}"), 16)
                sp.wait_ge(sem("b_x"), LEAD + i * SUP)
                if tiles == SUP:
                    sp.dma_start(base_in[:, :, :], baseD[bass.ds(i * (SUP * P), SUP * P), :].rearrange(
                        "(j p) n -> p j n", p=P)).then_inc(sem("bx_in"), 16)
                    sp.dma_start(x_in[:, :, :], x[bass.ds(i * (SUP * P), SUP * P), :].rearrange(
                        "(j p) n -> p j n", p=P)).then_inc(sem("bx_in"), 16)
                else:
                    sp.dma_start(base_in[:, 0, :], baseD[(TILES - 1) * P:TILES * P, :]).then_inc(sem("bx_in"), 16)
                    sp.wait_ge(sem("x_zero"), 1)
                    sp.dma_start(x_in[0:LAST, 0, :], x[(TILES - 1) * P:NODES, :]).then_inc(sem("bx_in"), 16)

            with sp.Fori(0, SUPERS) as i:
                load_super(i, SUP, P)
            load_super(SUPERS, 1, LAST)
            sp.wait_ge(sem("out_st"), DLEAD + 16 * (SUPERS + 1))

        @block.gpsimd
        def _(pool):
            dma_ahead(pool, "s_scat", len(LED_DMA))
            const = Chain(pool, "pool_const")

            def iota(o, pattern, cm=0):
                const(pool.iota(o, pattern, base=0, channel_multiplier=cm, allow_small_or_imprecise_dtypes=True))

            iota(iota16[:, :], [[1, GN]])
            iota(grow, [[1, SPAD]])
            iota(chunk_no[:, :], [[P, CB]], 1)
            iota(step_no[:, :], [[P, SB]], 1)
            for q in range(4):
                iota(relcol[32 * q:32 * q + 32, :], [[0, 1]], 1)
            pool.wait_ge(sem("dve_const"), 1)
            const(pool.affine_select(out=ident[:, :], in_=ident[:, :], compare_op=ALU.not_equal, fill=1.0, base=0,
                                     pattern=[[-1, P]], channel_multiplier=1))
            pool.wait_ge(sem("dve_const"), 8)
            const(pool.affine_select(out=rowmask[:, :], in_=rowmask[:, :], compare_op=ALU.is_gt, fill=0.0, base=NODES,
                                     pattern=[[-P, TILES]], channel_multiplier=-1))

            pool.wait_ge(sem("flag_ready"), 1)
            unsorted = pool.value_load(flag[0:1, 0:1], min_val=0, max_val=1)
            with pool.If(unsorted > 0):
                pool.iota(s_iota, [[1, SORTK]], base=0, channel_multiplier=0,
                          allow_small_or_imprecise_dtypes=True).then_inc(sem("s_const"), 1)
                pool.wait_ge(sem("s_lowone"), 1)
                pool.affine_select(out=s_low, in_=s_low, compare_op=ALU.is_gt, fill=0.0, base=0,
                                   pattern=[[1, P]], channel_multiplier=-1).then_inc(sem("s_const"), 1)
                with pool.Fori(0, CHUNKS) as i:
                    wait_apart(pool, "s_recs", i + 1)
                    pool.indirect_dma_start(out=srt, out_offset=bass.IndirectOffsetOnAxis(ap=s_idx, axis=0),
                                            in_=s_rec, in_offset=None).then_inc(sem("s_scat"), 16)

            pool.wait_ge(sem("rec_ready"), 1)
            with pool.Fori(0, SB // 4) as i:
                for u in range(4):
                    wait_apart(pool, "col_ready", i * 4 + u + 1)
                    pool.indirect_dma_start(out=irec[:, u, :], out_offset=None, in_=rec,
                                            in_offset=bass.IndirectOffsetOnAxis(ap=colc[:, u:u + 1], axis=0)
                                            ).then_inc(sem(f"irec_in{u}"), 16)
            pool.wait_ge(sem("xn_ready"), 1)

            def steps(it):
                for k in range(UN):
                    if k % RING == 0:
                        pool.wait_ge(sem("idx_ready"), 2 * it + k // RING + 1)
                    wait_apart(pool, "mm_done", it * UN + k + 1)
                    pool.indirect_dma_start(out=ring[:, k % RING, :], out_offset=None, in_=xnD,
                                            in_offset=bass.IndirectOffsetOnAxis(ap=idxc[:, k:k + 1], axis=0)
                                            ).then_inc(sem(f"row_in{k % RING}"), 16)

            with pool.Fori(0, ITERS) as it:
                steps(it)
            pool.nop().then_inc(sem("main_over"), 1)

        @block.scalar
        def _(act):
            start_ahead(act, "act")
            for q in range(4):
                act.wait_ge(sem("dve_const"), 3)
                act.dma_start(wblk[32 * q:32 * q + 32, BASES * q:BASES * (q + 1)], w_comp).then_inc(sem("w_in"), 16)
            act.dma_start(wq_s[:, :, :], rows(Wq, KH)).then_inc(sem("w_in"), 16)
            act.dma_start(wkv_s[:, :, 0:C], rows(Wk, KH)).then_inc(sem("w_in"), 16)
            act.dma_start(wkv_s[:, :, C:2 * C], rows(Wv, KH)).then_inc(sem("w_in"), 16)
            act.dma_start(wm_s[:, :, :], rows(Wm, KH)).then_inc(sem("w_in"), 16)
            act.dma_start(w1_s[:, :, :], rows(W1, 4)).then_inc(sem("w_in"), 16)
            act.dma_start(w2_s[:, :, :], rows(W2, 4)).then_inc(sem("w_in"), 16)
            for n, v in enumerate((g1, b1, g2, b2)):
                act.dma_start(lnw[:, n, :], v.rearrange("(a n) -> a n", a=1).to_broadcast([P, C])
                              ).then_inc(sem("w_in"), 16)
            act.dma_start(wr_s[:, :, :], rows(Wr, KH)).then_inc(sem("w_in"), 16)
            act.dma_start(br_s[:, :], br.rearrange("(a n) -> a n", a=1).to_broadcast([P, EXPERTS])
                          ).then_inc(sem("w_in"), 16)
            act.dma_start(bo_s[:, :], bo).then_inc(sem("w_in"), 16)
            for n, v in enumerate((fb1, fg1, fbe1, fm1, fv1, fb2, fg2, fbe2, fm2, fv2)):
                act.dma_start(bnrow[:, n, :], v.rearrange("e (k p) -> (e k) p", p=P)).then_inc(sem("bn_in"), 16)

            with act.Fori(0, LG) as i:
                for h in range(2):
                    at = i * (2 * LT * P) + h * LT * P
                    act.wait_ge(sem(f"ln_n{h}"), LT * (i + 1))
                    act.dma_start(xnD[bass.ds(at, LT * P), :].rearrange("(t p) n -> p t n", p=P), lnx[:, h, :, :]
                                  ).then_inc(sem(f"ln_st{h}"), 16)
            act.wait_ge(sem("ln_n0"), LT * LG + 1)
            act.dma_start(xnD[(TILES - 1) * P:TILES * P, :], lnx[:, 0, 0, :]).then_inc(sem("ln_st0"), 16)

            act.wait_ge(sem("bn_tp"), 1)
            act.copy(bnc[:, :, :].rearrange("p a e -> p (a e)"), bank(3, 0, 8 * EXPERTS)).then_inc(sem("bnc_ready"), 1)

            with act.Fori(0, SB // 4) as i:
                for u in range(4):
                    act.wait_ge(sem("fld_tp"), LEAD + 4 * i + u + 1)
                    act.copy(table[:, :, bass.ds((4 * i + u) * P, P)],
                             bank(u % 2, 0, 3 * P).rearrange("p (f e) -> p f e", f=3)).then_inc(sem("table_cp"), 1)
            act.wait_ge(sem("rec_ready"), 1)
            for t, w in ((f1_s, fW1), (f2_s, fW2), (fo_s, Wo)):
                for k in range(KH):
                    act.dma_start(t[:, :, k, :], w[:, k * P:(k + 1) * P, :].rearrange("e p n -> p e n")
                                  ).then_inc(sem("ffw_in"), 16)
            for k in range(KH):
                act.dma_start(bases_s[:, :, k, :], bases[:, k * P:(k + 1) * P, :].rearrange("b p n -> p b n")
                              ).then_inc(sem("ffw_in"), 16)

            with act.Fori(0, TILES) as i:
                act.wait_ge(sem("m1_tp"), i + 1)
                act.wait_ge(sem("m1_kv"), LEAD + i)
                act.copy(xnt[:, :, :].rearrange("p k n -> p (k n)"), bank(4, 0, C)).then_inc(sem("m1_xt"), 1)
                act.wait_ge(sem("m1_kv"), LEAD + i + 1)
                act.wait_ge(sem("m1_k"), LEAD + i)
                act.activation(ek[:, :], bank(5, 0, C), ACT.Exp).then_inc(sem("m1_parts"), 1)
                act.activation(rk[:, :], bank(5, 0, C), ACT.Relu).then_inc(sem("m1_parts"), 1)
                act.wait_ge(sem("m1_acc"), LEAD + i)
                act.activation(vx[:, :, 0:P], bank(5, C, 2 * C).rearrange("p (k n) -> p k n", k=KH), ACT.Copy,
                               scale=1.0 / NODES).then_inc(sem("m1_v"), 1)
                act.copy(vx[:, :, P:P + 1], rowmask[:, bass.ds(i, 1)].unsqueeze(1).to_broadcast([P, KH, 1])
                         ).then_inc(sem("m1_v"), 1)
            with act.Fori(0, TILES) as i:
                act.wait_ge(sem("m2_tp"), i + 1)
                act.wait_ge(sem("m2_w1"), LEAD + i)
                act.copy(cat[:, 0:KH, :].rearrange("p k n -> p (k n)"), bank(4, 0, C)).then_inc(sem("m2_xt"), 1)
                act.wait_ge(sem("m2_q"), i + 1)
                act.wait_ge(sem("m2_qt"), LEAD + i)
                act.activation(ek[:, :], bank(5, 0, C), ACT.Exp).then_inc(sem("m2_parts"), 1)
                act.activation(rk[:, :], bank(5, 0, C), ACT.Relu).then_inc(sem("m2_parts"), 1)
                act.wait_ge(sem("m2_tm"), LEAD + i + 1)
                act.wait_ge(sem("m2_wm"), LEAD + i)
                act.copy(mst[:, :, :].rearrange("p k n -> p (k n)"), bank(4, 0, C)).then_inc(sem("m2_mt"), 1)
                act.wait_ge(sem("m2_tn"), LEAD + i + 1)
                act.copy(cat[:, KH:2 * KH, :].rearrange("p k n -> p (k n)"), bank(4, 0, C)).then_inc(sem("m2_nt"), 1)
                act.wait_ge(sem("m2_w1"), LEAD + i + 1)
                act.wait_ge(sem("m2_w2"), LEAD + i)
                act.activation(ht[:, :, :].rearrange("p k n -> p (k n)"), bank(7), ACT.Relu).then_inc(sem("m2_h"), 1)
                act.wait_ge(sem("m2_base"), LEAD + i + 1)
                act.dma_start(baseD[bass.ds(i * P, P), :], mo[:, 3, :]).then_inc(sem("base_out"), 16)
            act.nop().then_inc(sem("main_over"), 1)

            def super_act(i, tiles):
                n = tiles * P
                for j in range(tiles):
                    act.wait_ge(sem("b_tp"), LEAD + i * SUP + j + 1)
                    if j == 0:
                        act.wait_ge(sem("f_l1"), LEAD + EXPERTS * i)
                    act.copy(x1t[:, :, j * P:(j + 1) * P], bank(6 + j % 2, C, 2 * C).rearrange(
                        "p (k n) -> p k n", k=KH)).then_inc(sem("b_xt"), 1)
                act.wait_ge(sem("r_sub"), i + 1)
                act.activation(ex[:, 0:tiles * EXPERTS], lg[:, 0:tiles * EXPERTS], ACT.Exp).then_inc(sem("r_exp"), 1)
                act.wait_ge(sem("r_tp"), i + 1)
                act.copy(wt[:, 0:n], bank(4, 0, n)[0:EXPERTS, :]).then_inc(sem("r_wt"), 1)

                def hidden(e, layer):
                    o, b0, s = ((h1, 0, "1"), (h2, 2, "2"))[layer]
                    act.wait_ge(sem(f"f_l{s}"), LEAD + EXPERTS * i + e + 1)
                    if layer == 0:
                        act.wait_ge(sem("f_l2"), LEAD + EXPERTS * i + e)
                    else:
                        act.wait_ge(sem("f_l3"), LEAD + SUP * EXPERTS * i + tiles * e)
                    for k in range(KH):
                        act.activation(o[:, k, 0:n], bank(b0 + k, 0, n), ACT.Relu,
                                       bias=bnc[:, 2 * layer + 1, 2 * e + k:2 * e + k + 1],
                                       scale=bnc[:, 2 * layer, 2 * e + k:2 * e + k + 1]).then_inc(sem(f"f_h{s}"), 1)

                for e in range(EXPERTS):
                    hidden(e, 0)
                    hidden(e, 1)
                act.wait_ge(sem("o_upd"), LEAD + SUP * (EXPERTS + 1) * i + tiles * (EXPERTS + 1))
                if tiles == SUP:
                    act.dma_start(out[bass.ds(i * (SUP * P), SUP * P), :].rearrange("(j p) n -> p j n", p=P),
                                  oacc[:, :, :]).then_inc(sem("out_st"), 16)
                else:
                    act.dma_start(out[(TILES - 1) * P:NODES, :], oacc[0:LAST, 0, :]).then_inc(sem("out_st"), 16)

            with act.Fori(0, SUPERS) as i:
                super_act(i, SUP)
            super_act(SUPERS, 1)

        @block.vector
        def _(dve):
            def tt(o, a, b, op):
                return dve.tensor_tensor(o, a, b, op)

            def rsqrt(link, var, eps, n=P, shape=None):
                w = var.shape[-1]
                v, y, t, u = (nrw[0:n, k, 0:w] for k in range(4))
                link(dve.tensor_scalar(v, var, eps, None, ALU.add))
                link(dve.tensor_scalar(nri[0:n, 0:w], v.bitcast(I32), 1, None, ALU.logical_shift_right))
                link(dve.tensor_scalar(y.bitcast(I32), nri[0:n, 0:w], -1.0, float(RSQRT_SEED), ALU.mult, ALU.add))
                for _ in range(NEWTON):
                    if w == 1:
                        link(dve.scalar_tensor_tensor(t, y, v, y, ALU.mult, ALU.mult))
                    else:
                        link(tt(t, y, y, ALU.mult))
                        link(tt(t, t, v, ALU.mult))
                    link(dve.tensor_scalar(u, t, -0.5, 1.5, ALU.mult, ALU.add))
                    link(tt(y, y, u, ALU.mult))
                return y

            start_ahead(dve, "dve")
            dve.memset(ident[:, :], 0.0).then_inc(sem("dve_const"), 1)
            dve.memset(chk_b[:, CHKN - 1:CHKN], FAR).then_inc(sem("dve_const"), 1)
            dve.memset(wblk[:, :], 0.0).then_inc(sem("dve_const"), 1)
            dve.memset(padc[:, :], 0).then_inc(sem("dve_const"), 1)
            dve.wait_ge(sem("dve_const"), 4)
            dve.memset(padc[:, PADE:2 * PADE], FAR).then_inc(sem("dve_const"), 1)
            dve.memset(zrow[:, :], 0.0).then_inc(sem("dve_const"), 1)
            dve.memset(fdst[:, :], FAR).then_inc(sem("dve_const"), 1)
            dve.memset(rowmask[:, :], 1.0).then_inc(sem("dve_const"), 1)
            dve.memset(ones[:, :], 1.0).then_inc(sem("dve_const"), 1)
            dve.memset(kvmask[:, :], 0.0).then_inc(sem("dve_const"), 1)
            dve.memset(headmask[:, :], 0.0).then_inc(sem("dve_const"), 1)
            dve.wait_ge(sem("dve_const"), 11)
            for q in range(4):
                b = slice(HD * q, HD * (q + 1))
                dve.memset(kvmask[b, b], 1.0).then_inc(sem("dve_const"), 1)
                dve.memset(headmask[b, q:q + 1], 1.0).then_inc(sem("dve_const"), 1)

            link = Chain(dve, "dve_chain")
            dve.wait_ge(sem("chk_in"), 48)
            link(tt(chk_c, chk_a, chk_b, ALU.is_gt))
            dve.tensor_reduce(flagf[0:CHKP, :], chk_c, AX.X, ALU.max).then_inc(sem("chk_max"), 1)
            dve.wait_ge(sem("chk_sum"), 1)
            dve.tensor_scalar(flag[:, :], bank(2, 0, 1)[0:1, :], 0.0, None, ALU.is_gt).then_inc(sem("flag_ready"), 1)

            dve.wait_ge(sem("bn_in"), 160)
            for l in range(2):
                b_, g_, be_, m_, v_ = (bnrow[:, 5 * l + n, :] for n in range(5))
                y = rsqrt(link, v_, BN_EPS, 2 * EXPERTS)
                link(tt(bnt[:, 2 * l, :], g_, y, ALU.mult))
                link(tt(bnd, b_, m_, ALU.subtract))
                link(tt(bnd, bnd, bnt[:, 2 * l, :], ALU.mult))
                link(tt(bnt[:, 2 * l + 1, :], bnd, be_, ALU.add))
            tt(bnd, bnd, bnd, ALU.mult).then_inc(sem("bn_folded"), 1)

            NORM = 2 * LT + 3 + 4 * NEWTON
            ln0 = link.n

            def normalise(h, tiles, count):
                for t in range(tiles):
                    link(dve.bn_stats(lns[:, t, :], lnx[:, h, t, :]), apart=True)
                    link(dve.bn_aggr(lnmv[:, t, :], lns[:, t, :]))
                y = rsqrt(link, lnmv[:, 0:tiles, 1], LN_EPS)
                for t in range(tiles):
                    dve.tensor_scalar(lnx[:, h, t, :], lnx[:, h, t, :], lnmv[:, t, 0:1], y[:, t:t + 1],
                                      ALU.subtract, ALU.mult).then_inc(sem(f"ln_n{h}"), 1)
                dve.wait_ge(sem(f"ln_n{h}"), count)

            with dve.Fori(0, LG) as i:
                link.n = ln0 + i * (2 * NORM)
                for h in range(2):
                    dve.wait_ge(sem(f"ln_ld{h}"), 16 * (i + 1))
                    normalise(h, LT, LT * (i + 1))
            link.n = ln0 + LG * 2 * NORM
            dve.wait_ge(sem("ln_st0"), DLEAD + 16 * LG)
            dve.memset(lnx[:, 0, 0, :], 0.0).then_inc(sem("ln_zero"), 1)
            dve.wait_ge(sem("ln_ld0"), 16 * (LG + 1))
            normalise(0, 1, LT * LG + 1)

            dve.wait_ge(sem("flag_ready"), 1)
            unsorted = dve.value_load(flag[0:1, 0:1], min_val=0, max_val=1)
            with dve.If(unsorted > 0):
                real = EDGES - (P - 1) * CHUNKS
                dve.memset(s_dst[:, real:CHUNKS], FAR).then_inc(sem("s_fill"), 1)
                dve.memset(s_oth[:, :, real:CHUNKS], 0).then_inc(sem("s_fill"), 1)
                dve.memset(s_all, 1.0).then_inc(sem("s_const"), 1)
                dve.memset(s_low, 1.0).then_inc(sem("s_lowone"), 1)
                dve.memset(s_run, 0.0).then_inc(sem("s_const"), 1)
                dve.wait_ge(sem("s_in"), 128)
                dve.wait_ge(sem("s_const"), 4)
                slink = Chain(dve, "s_chain")
                slink(dve.tensor_scalar(s_rank.bitcast(I32), s_dst, 4, None, ALU.logical_shift_right))
                slink(dve.tensor_scalar(s_key, s_rank.bitcast(I32), float(SORTK - 1), None, ALU.min))

                def one_hot(i):
                    slink(dve.tensor_scalar(s_one, s_iota, s_key[:, bass.ds(i, 1)], None, ALU.is_equal))

                RANK = 6
                with dve.Fori(0, CHUNKS) as i:
                    slink.n = i * RANK + 2
                    one_hot(i)
                    dve.wait_ge(sem("s_mm"), i + 1)
                    slink(tt(s_tmp, bank(0, 0, SORTK), s_run, ALU.add))
                    slink(tt(s_tmp, s_tmp, s_one, ALU.mult))
                    slink(dve.tensor_reduce(s_col[:, 0:1], s_tmp, AX.X, ALU.add))
                    slink(dve.tensor_copy(s_rank[:, bass.ds(i, 1)], s_col[:, 0:1]))
                    slink(tt(s_run, s_run, bank(1, 0, SORTK), ALU.add))
                slink.n = CHUNKS * RANK + 2
                slink(dve.memset(s_start, 1.0))
                slink(dve.tensor_tensor_scan(s_tmp, s_start, s_run, 0.0, ALU.mult, ALU.add))
                slink(tt(s_start, s_tmp, s_run, ALU.subtract))
                PLACE = 8
                with dve.Fori(0, CHUNKS) as i:
                    slink.n = i * PLACE + CHUNKS * RANK + 5
                    one_hot(i)
                    slink(tt(s_tmp, s_start, s_one, ALU.mult))
                    slink(dve.tensor_reduce(s_col[:, 0:1], s_tmp, AX.X, ALU.add))
                    dve.wait_ge(sem("s_scat"), DLEAD + 16 * i)
                    slink(tt(s_idx, s_col[:, 0:1], s_rank[:, bass.ds(i, 1)], ALU.add))
                    slink(dve.tensor_copy(s_rec[:, 0:1], s_oth[:, 0, bass.ds(i, 1)]))
                    slink(dve.tensor_copy(s_rec[:, 1:2], s_dst[:, bass.ds(i, 1)]))
                    slink(dve.tensor_copy(s_rec[:, 2:3], s_oth[:, 1, bass.ds(i, 1)]))
                    slink(dve.tensor_copy(s_rec[:, 3:4].bitcast(F32), s_oth[:, 2, bass.ds(i, 1)].bitcast(F32)))
                    dve.nop().then_inc(sem("s_recs"), 1)
                for j in range(CB):
                    n = P if j < CB - 1 else CREST
                    dve.wait_ge(sem("s_rin"), 16 * (j + 1))
                    frm = s_blk[0:n, 0, :].rearrange("p (e f) -> p f e", f=4)
                    to = s_blk[0:n, 1, :].rearrange("p (f e) -> p f e", f=4)
                    dve.tensor_copy(to[:, 0:3, :], frm[:, 0:3, :]).then_inc(sem("s_turn"), 1)
                    dve.tensor_copy(to[:, 3, :].bitcast(F32), frm[:, 3, :].bitcast(F32)).then_inc(sem("s_turn"), 1)

            dve.wait_ge(sem("fdst_in"), 32)
            dve.wait_ge(sem("pool_const"), 10)
            link(dve.tensor_scalar(fgrp[:, :], fdst[:, :], 4, None, ALU.logical_shift_right))
            link(tt(tcol[:, :], fgrp[:, :], chunk_no[:, :], ALU.add))
            link(dve.memset(tcol[0:1, 0:1], float(4 * SPAD)))
            for j in range(CB):
                if j >= 2:
                    dve.wait_ge(sem("spread"), j - 1)
                dve.tensor_scalar(diag[:, j % 2, :], ident[:, :], tcol[:, j:j + 1], None, ALU.mult
                                  ).then_inc(sem("diag_ready"), 1)
            dve.wait_ge(sem("spread"), CB)
            for j in range(SB):
                dve.tensor_scalar(junk, PS[:, 4 * 512:4 * 512 + CB * P], step_no[:, j:j + 1], 0.0,
                                  ALU.is_le, ALU.add, accum_out=cstep[:, j:j + 1]).then_inc(sem("cstep_ready"), 1)
                dve.wait_ge(sem("cstep_ready"), j + 1)
            link(dve.tensor_copy(cint[:, :], cstep[:, :]))
            link(dve.scalar_tensor_tensor(gbase[:, 0, :], cstep[:, :], -1.0, step_no[:, :], ALU.mult, ALU.add))
            link(dve.tensor_scalar(gbase[:, 1, :], gbase[:, 0, :], float(GN), None, ALU.mult))
            dve.wait_ge(sem("crow_in"), 16)
            link(dve.memset(crow[:, 0:1], 0.0))
            dve.tensor_tensor(keep, crow[:, 1:SPAD + 1], crow[:, 0:SPAD], ALU.subtract).then_inc(sem("tables_ready"), 1)
            dve.wait_ge(sem("tables_ready"), 1)
            dve.scalar_tensor_tensor(grow, crow[0:1, 1:SPAD + 1], -1.0, grow, ALU.mult, ALU.add
                                     ).then_inc(sem("tables_ready"), 1)
            with dve.Fori(0, SB // 4) as i:
                dve.wait_ge(sem("fld_tp"), LEAD + 4 * i)
                for u in range(4):
                    dve.tensor_copy(colc[:, u:u + 1], cint[:, bass.ds(4 * i + u, 1)]).then_inc(sem("col_ready"), 1)
                    dve.tensor_copy(colg[:, u:u + 1], gbase[:, 1, bass.ds(4 * i + u, 1)]).then_inc(sem("colg_ready"), 1)
                dve.wait_ge(sem("colg_ready"), 4 * i + 4)
                for u in range(4):
                    dve.wait_ge(sem(f"irec_in{u}"), 16 * (i + 1))
                    dve.wait_ge(sem(f"rels_out{u}"), DLEAD + 16 * i)
                    dve.tensor_copy(ifld[:, u, 0, :], irec[:, u, 0:P]).then_inc(sem("fld_ready"), 1)
                    dve.tensor_scalar(ifld[:, u, 1, :], irec[:, u, P:2 * P], colg[:, u:u + 1], None, ALU.subtract
                                      ).then_inc(sem("fld_ready"), 1)
                    dve.tensor_copy(ifld[:, u, 2, :], irec[:, u, 2 * P:3 * P]).then_inc(sem("fld_type"), 1)

            def rel_hot(it):
                dve.wait_ge(sem("types_in"), 64 * (it + 1))
                dve.wait_ge(sem("coef_mm"), LEAD + it)
                dve.tensor_scalar(relhot, relb, relcol[:, 0:1], None, ALU.is_equal).then_inc(sem("relhot_ready"), 1)

            def dst_hot(it):
                dve.wait_ge(sem("sel_ready"), LEAD + NB * it)
                dve.tensor_tensor(hot, table[:, 1, bass.ds(it * UN, UN)].unsqueeze(2).to_broadcast([P, UN, GN]),
                                  iota16[:, :].unsqueeze(1).to_broadcast([P, UN, GN]), ALU.is_equal
                                  ).then_inc(sem("hot_ready"), 1)

            def coefs(it):
                dve.wait_ge(sem("coef_mm"), LEAD + it + 1)
                dve.tensor_tensor(coef, bank(6, 0, UN * BASES).rearrange("p (s b) -> p s b", b=BASES),
                                  table[:, 2, bass.ds(it * UN, UN)].unsqueeze(2).to_broadcast([P, UN, BASES]), ALU.mult
                                  ).then_inc(sem("coef_ready"), 1)

            def select(it, q, free):
                dve.wait_ge(sem("hot_ready"), it + 1)
                dve.wait_ge(sem("coef_ready"), LEAD + it + 1)
                dve.wait_ge(sem("mm_done"), free)
                s = slice(q * BATCH, (q + 1) * BATCH)
                dve.tensor_tensor(selm[:, q % 2, :, :, :],
                                  hot[:, s, :].unsqueeze(3).to_broadcast([P, BATCH, GN, BASES]),
                                  coef[:, s, :].unsqueeze(2).to_broadcast([P, BATCH, GN, BASES]), ALU.mult
                                  ).then_inc(sem("sel_ready"), 1)

            def indices(it, h):
                dve.tensor_copy(idxc[:, h * RING:(h + 1) * RING], table[:, 0, bass.ds(it * UN + h * RING, RING)]
                                ).then_inc(sem("idx_ready"), 1)

            def keeps(it):
                dve.tensor_copy(keepc, keep[:, bass.ds(it * UN, UN)]).then_inc(sem("keepc_ready"), 1)

            dve.wait_ge(sem("table_cp"), LEAD + SB)
            dve.wait_ge(sem("tables_ready"), 2)
            for u in range(4):
                dve.wait_ge(sem(f"rels_out{u}"), DLEAD + 16 * (SB // 4))
            rel_hot(0)
            dst_hot(0)
            coefs(0)
            dve.wait_ge(sem("mm_credit"), 1)
            select(0, 0, RING)
            indices(0, 0)
            keeps(0)
            dve.memset(acc[:, RING - 1, :], 0.0).then_inc(sem("acc_zero"), 1)
            dve.wait_ge(sem("acc_zero"), 1)
            dve.sem_inc(sem("acc_done"), SLOTS)

            def steps(it, extra):
                for k in range(UN):
                    s = it * UN + k
                    if k == 0:
                        select(it, 1, it * UN + RING)
                        indices(it, 1)
                        dve.wait_ge(sem("keepc_ready"), it + 1)
                    if k == BATCH:
                        select(it, 2, it * UN + BATCH + RING)
                    if k == 7:
                        rel_hot(it + 1)
                    if k == 2 * BATCH:
                        select(it, 3, it * UN + 2 * BATCH + RING)
                        indices(it + 1, 0)
                    if k == 12:
                        dst_hot(it + 1)
                    if k == 13:
                        coefs(it + 1)
                    if k == 3 * BATCH:
                        select(it + 1, 0, it * UN + 3 * BATCH + RING)
                    dve.wait_ge(sem("mm_done"), s + 1 + RING)
                    dve.wait_ge(sem("acc_done"), s + SLOTS)
                    dve.wait_ge(sem(f"flush{k % RING}"), DLEAD + 32 * it + 16 * (k // RING))
                    a = (k % SLOTS) * 512
                    dve.scalar_tensor_tensor(acc[:, k % RING, :], acc[:, (k - 1) % RING, :], keepc[:, k:k + 1],
                                             PS[:, a:a + C], ALU.mult, ALU.add).then_inc(sem("acc_done"), 1)
                    if k in extra:
                        extra[k]()
                dve.wait_ge(sem("acc_done"), (it + 1) * UN + SLOTS)
                keeps(it + 1)

            with dve.Fori(0, TILES) as i:
                def m1_k():
                    dve.wait_ge(sem("m1_parts"), 2 * i + 2)
                    dve.wait_ge(sem("m1_acc"), LEAD + i)
                    dve.scalar_tensor_tensor(ksb, ek, 1.0, rk, ALU.min, ALU.add).then_inc(sem("m1_k"), 1)
                steps(i, {8: m1_k})

            dve.wait_ge(sem("m1_acc"), LEAD + TILES)
            for h in range(KH):
                a = h * (P + 1)
                tt(kvb[:, h, 0:P], bank(7, a, a + P), kvmask[:, :], ALU.mult).then_inc(sem("kvb_ready"), 1)
                dve.tensor_scalar(kvb[:, h, P:P + 4], headmask[:, :], bank(7, a + P, a + P + 1), None, ALU.mult
                                  ).then_inc(sem("kvb_ready"), 1)

            NORM1 = 2 + 3 + 3 * NEWTON
            MIXED = 2 + 2 * NORM1 + 3
            mix0 = link.n

            def mix_norm(ps, o, g, b, done):
                link(dve.bn_stats(lst[:, :], ps), apart=True)
                link(dve.bn_aggr(lmv[:, :], lst[:, :]))
                y = rsqrt(link, lmv[:, 1:2], LN_EPS)
                dve.tensor_scalar(o[:, 0, :], ps, lmv[:, 0:1], y, ALU.subtract, ALU.mult).then_inc(sem(done), 1)

            with dve.Fori(0, TILES) as i:
                def m2_q():
                    dve.wait_ge(sem("m2_parts"), 2 * i + 2)
                    dve.wait_ge(sem("m2_msg"), LEAD + i)
                    dve.scalar_tensor_tensor(qt[:, :, :].rearrange("p k n -> p (k n)"), ek, 1.0, rk, ALU.min, ALU.add
                                             ).then_inc(sem("m2_qt"), 1)

                num = bank(7, 0, 2 * (P + 4)).rearrange("p (k n) -> p k n", k=KH)

                def m2_z():
                    dve.wait_ge(sem("m2_msg"), LEAD + i + 1)
                    link.n = mix0 + i * MIXED
                    link(dve.tensor_scalar(zt[:, :].rearrange("p (k n) -> p k n", k=KH), num[:, :, P:P + 4], ATT_EPS,
                                           None, ALU.add))
                    link(dve.reciprocal(zi[:, :], zt[:, :]))

                def m2_m():
                    dve.wait_ge(sem("m2_tm"), LEAD + i)
                    for k in range(KH):
                        dve.scalar_tensor_tensor(
                            msb[:, k * P:(k + 1) * P].rearrange("p (h v) -> p h v", v=HD),
                            num[:, k, 0:P].rearrange("p (h v) -> p h v", v=HD), float(NODES),
                            zi[:, 4 * k:4 * k + 4].unsqueeze(2).to_broadcast([P, 4, HD]), ALU.mult, ALU.mult
                        ).then_inc(sem("m2_mm"), 1)

                def m2_ln1():
                    dve.wait_ge(sem("m2_wm"), LEAD + i + 1)
                    mix_norm(bank(5, 0, C), mn, 0, 1, "m2_1n")

                def m2_g1():
                    dve.wait_ge(sem("m2_1n"), i + 1)
                    link(tt(mn[:, 1, :], mn[:, 0, :], lnw[:, 0, :], ALU.mult))
                    dve.wait_ge(sem("m2_tn"), LEAD + i)
                    tt(mn[:, 2, :], mn[:, 1, :], lnw[:, 1, :], ALU.add).then_inc(sem("m2_1b"), 1)

                def m2_ln2():
                    dve.wait_ge(sem("m2_w2"), LEAD + i + 1)
                    mix_norm(bank(5, 0, C), mo, 2, 3, "m2_2n")
                    dve.wait_ge(sem("m2_2n"), LEAD + i + 1)
                    link(tt(mo[:, 1, :], mo[:, 0, :], lnw[:, 2, :], ALU.mult))
                    link(tt(mo[:, 2, :], mo[:, 1, :], lnw[:, 3, :], ALU.add))
                    dve.wait_ge(sem("xr2_in"), 16 * (i + 1))
                    dve.wait_ge(sem("base_out"), DLEAD + 16 * i)
                    tt(mo[:, 3, :], mo[:, 2, :], xr2, ALU.add).then_inc(sem("m2_base"), 1)

                steps(i + TILES, {4: m2_q, 7: m2_z, 8: m2_m, 12: m2_ln1, 13: m2_g1, 19: m2_ln2})
            dve.nop().then_inc(sem("main_over"), 1)

            link.n = ff0 = mix0 + TILES * MIXED
            dve.wait_ge(sem("main_over"), 4)
            for r in range(RING):
                dve.wait_ge(sem(f"flush{r}"), DLEAD + 16 * ITERS * UN // RING)
            FNORM = 2 * SUP + 3 + 4 * NEWTON + 4

            def super_dve(i, tiles):
                if tiles < SUP:
                    dve.wait_ge(sem("b_x"), LEAD + SUPERS * SUP)
                    dve.memset(x_in[:, 0, :], 0.0).then_inc(sem("x_zero"), 1)
                link.n = ff0 + i * FNORM
                dve.wait_ge(sem("bx_in"), 32 * (i + 1))
                for j in range(tiles):
                    dve.wait_ge(sem("b_mm"), LEAD + i * SUP + j + 1)
                    dve.scalar_tensor_tensor(xr[:, j, :], bank(6 + j % 2, 0, C), 0.0, base_in[:, j, :], ALU.max, ALU.add
                                             ).then_inc(sem("b_r"), 1)
                    dve.wait_ge(sem("b_r"), LEAD + i * SUP + j + 1)
                    tt(x1[:, j, :], xr[:, j, :], x_in[:, j, :], ALU.add).then_inc(sem("b_x"), 1)
                    dve.wait_ge(sem("b_x"), LEAD + i * SUP + j + 1)
                    link(dve.bn_stats(bst[:, j, :], x1[:, j, :]), apart=True)
                    link(dve.bn_aggr(bmv[:, j, :], bst[:, j, :]))
                y = rsqrt(link, bmv[:, 0:tiles, 1], LN_EPS)
                dve.wait_ge(sem("b_tp"), LEAD + i * SUP)
                for j in range(tiles):
                    dve.tensor_scalar(x1n[:, j, :], x1[:, j, :], bmv[:, j, 0:1], y[:, j:j + 1], ALU.subtract, ALU.mult
                                      ).then_inc(sem("b_n"), 1)
                n = tiles * EXPERTS

                def per(t):
                    return t[:, 0:n].rearrange("p (j e) -> p j e", e=EXPERTS)

                def wide(t):
                    return t[:, 0:tiles].unsqueeze(2).to_broadcast([P, tiles, EXPERTS])

                dve.wait_ge(sem("r_lg"), i + 1)
                link(tt(per(ex), bank(5, 0, n).rearrange("p (j e) -> p j e", e=EXPERTS),
                   br_s[:, :].unsqueeze(1).to_broadcast([P, tiles, EXPERTS]), ALU.add))
                link(dve.tensor_reduce(rmx[:, 0:tiles], per(ex), AX.X, ALU.max))
                tt(per(lg), per(ex), wide(rmx), ALU.subtract).then_inc(sem("r_sub"), 1)
                dve.wait_ge(sem("r_exp"), i + 1)
                link(dve.tensor_reduce(rsm[:, 0:tiles], per(ex), AX.X, ALU.add))
                link(dve.reciprocal(rin[:, 0:tiles], rsm[:, 0:tiles]))
                tt(per(rw), per(ex), wide(rin), ALU.mult).then_inc(sem("r_w"), 1)
                dve.wait_ge(sem("r_w"), i + 1)
                o0 = SUP * (EXPERTS + 1) * i
                dve.wait_ge(sem("out_st"), DLEAD + 16 * i)
                dve.wait_ge(sem("f_bo"), i + 1)
                for j in range(tiles):
                    tt(oacc[:, j, :], bank(4 + j // 2, (j % 2) * C, (j % 2) * C + C), x1[:, j, :], ALU.add
                       ).then_inc(sem("o_upd"), 1)
                for e in range(EXPERTS):
                    for j in range(tiles):
                        dve.wait_ge(sem("f_l3"), LEAD + SUP * EXPERTS * i + tiles * e + min(j // 2 * 2 + 2, tiles))
                        dve.wait_ge(sem("o_upd"), LEAD + o0 + tiles * e + j + 1)
                        dve.scalar_tensor_tensor(oacc[:, j, :], bank(4 + j // 2, (j % 2) * C, (j % 2) * C + C),
                                                 rw[:, EXPERTS * j + e:EXPERTS * j + e + 1], oacc[:, j, :],
                                                 ALU.mult, ALU.add).then_inc(sem("o_upd"), 1)

            with dve.Fori(0, SUPERS) as i:
                super_dve(i, SUP)
            super_dve(SUPERS, 1)

        @block.tensor
        def _(pe):
            def mm(o, a, b, start=True, stop=True):
                return pe.matmul(o, a, b, start=start, stop=stop)

            start_ahead(pe, "pe")
            pe.wait_ge(sem("dve_const"), 19)
            pe.wait_ge(sem("pool_const"), 10)
            pe.wait_ge(sem("chk_max"), 1)
            mm(bank(2, 0, 1)[0:1, :], flagf[0:CHKP, :], ones[0:CHKP, 0:1]).then_inc(sem("chk_sum"), 1)
            pe.wait_ge(sem("bn_folded"), 1)
            for a in range(4):
                last = pe.transpose(bank(3, 2 * EXPERTS * a, 2 * EXPERTS * (a + 1)), bnt[:, a, :],
                                    ident[0:2 * EXPERTS, 0:2 * EXPERTS])
            last.then_inc(sem("bn_tp"), 1)

            pe.wait_ge(sem("flag_ready"), 1)
            unsorted = pe.value_load(flag[0:1, 0:1], min_val=0, max_val=1)
            with pe.If(unsorted > 0):
                pe.wait_ge(sem("s_const"), 4)
                with pe.Fori(0, CHUNKS) as i:
                    pe.wait_ge(sem("s_chain"), i * 6 + 3)
                    mm(bank(0, 0, SORTK), s_low, s_one)
                    mm(bank(1, 0, SORTK), s_all, s_one).then_inc(sem("s_mm"), 1)

            for j in range(CB):
                pe.wait_ge(sem("diag_ready"), j + 1)
                mm(PS[:, 4 * 512 + j * P:4 * 512 + (j + 1) * P], ones[:, :], diag[:, j % 2, :]
                   ).then_inc(sem("spread"), 1)
            with pe.Fori(0, SB // 4) as i:
                for u in range(4):
                    pe.wait_ge(sem("fld_ready"), 2 * (4 * i + u + 1))
                    pe.wait_ge(sem("table_cp"), LEAD + 4 * i + (u - 1 if u >= 2 else 0))
                    b = bank(u % 2)
                    pe.transpose(b[:, 0:P], ifld[:, u, 0, :], ident[:, :])
                    pe.transpose(b[:, P:2 * P], ifld[:, u, 1, :], ident[:, :])
                    pe.transpose(b[:, 2 * P:3 * P], irec[:, u, 3 * P:4 * P].bitcast(F32), ident[:, :]
                                 ).then_inc(sem("fld_tp"), 1)

            def coef_mm(it):
                pe.wait_ge(sem("relhot_ready"), it + 1)
                pe.wait_ge(sem("coef_ready"), LEAD + it)
                for j in range(BATCH):
                    last = mm(bank(6, 4 * BASES * j, 4 * BASES * (j + 1)), relhot[:, j, :], wblk[:, :])
                last.then_inc(sem("coef_mm"), 1)

            pe.wait_ge(sem("w_in"), 16 * 17)
            pe.wait_ge(sem("bnc_ready"), 1)
            pe.wait_ge(sem("table_cp"), LEAD + SB)
            mm(bank(7, 0, KH * (P + 1)), zrow[:, 0:P], zrow[:, :])
            coef_mm(0)
            pe.sem_inc(sem("mm_done"), RING)
            pe.sem_inc(sem("mm_credit"), 1)

            def steps(it, extra):
                for k in range(UN):
                    s = it * UN + k
                    if k % BATCH == 0:
                        pe.wait_ge(sem("sel_ready"), LEAD + NB * it + k // BATCH + 1)
                    if k == 9:
                        coef_mm(it + 1)
                    pe.wait_ge(sem(f"row_in{k % RING}"), 32 * it + 16 * (k // RING) + 16)
                    pe.wait_ge(sem("acc_done"), s + 1)
                    a = (k % SLOTS) * 512
                    sel = selm[:, (k // BATCH) % 2, k % BATCH, :, :].rearrange("p n b -> p (n b)")
                    for h in range(KH):
                        last = mm(PS[:, a + h * P:a + (h + 1) * P], ring[:, k % RING, h * P:(h + 1) * P], sel)
                    last.then_inc(sem("mm_done"), 1)
                    if k in extra:
                        extra[k]()

            def turn(o, frm, name):
                for h in range(KH):
                    last = pe.transpose(o[:, h * P:(h + 1) * P], frm[:, h * P:(h + 1) * P], ident[:, :])
                last.then_inc(sem(name), 1)

            with pe.Fori(0, TILES) as i:
                def m1_turn():
                    pe.wait_ge(sem("xt_in"), 16 * (i + 1))
                    pe.wait_ge(sem("m1_xt"), LEAD + i)
                    turn(bank(4), xt, "m1_tp")

                def m1_kv():
                    pe.wait_ge(sem("m1_xt"), LEAD + i + 1)
                    pe.wait_ge(sem("m1_v"), LEAD + 2 * i)
                    for h in range(KH):
                        last = mm(bank(5), xnt[:, h, :], wkv_s[:, h, :], h == 0, h == KH - 1)
                    last.then_inc(sem("m1_kv"), 1)

                def m1_acc():
                    pe.wait_ge(sem("m1_k"), LEAD + i + 1)
                    pe.wait_ge(sem("m1_v"), LEAD + 2 * i + 2)
                    for h in range(KH):
                        a = h * (P + 1)
                        last = pe.matmul(bank(7, a, a + P + 1), ksb[:, h * P:(h + 1) * P], vx[:, h, :],
                                         start=False, stop=False, skip_group_check=True)
                    last.then_inc(sem("m1_acc"), 1)
                steps(i, {1: m1_turn, 4: m1_kv, 10: m1_acc})
            pe.wait_ge(sem("kvb_ready"), 2 * KH)
            pe.wait_ge(sem("m1_v"), LEAD + 2 * TILES)
            with pe.Fori(0, TILES) as i:
                def m2_turn():
                    pe.wait_ge(sem("xt_in"), 16 * (i + TILES + 2))
                    pe.wait_ge(sem("m2_nt"), LEAD + i)
                    turn(bank(4), xt, "m2_tp")

                def m2_q():
                    pe.wait_ge(sem("m2_xt"), i + 1)
                    pe.wait_ge(sem("m2_2n"), LEAD + i)
                    for o in range(KH):
                        for h in range(KH):
                            last = mm(bank(5, o * P, (o + 1) * P), wq_s[:, h, o * P:(o + 1) * P], cat[:, h, :],
                                      h == 0, h == KH - 1)
                    last.then_inc(sem("m2_q"), 1)

                def m2_msg():
                    pe.wait_ge(sem("m2_qt"), LEAD + i + 1)
                    pe.wait_ge(sem("m2_h"), LEAD + i)
                    for h in range(KH):
                        last = mm(bank(7, h * (P + 4), (h + 1) * (P + 4)), qt[:, h, :], kvb[:, h, :])
                    last.then_inc(sem("m2_msg"), 1)

                def m2_tm():
                    pe.wait_ge(sem("m2_mm"), KH * (i + 1))
                    turn(bank(4), msb, "m2_tm")

                def m2_wm():
                    pe.wait_ge(sem("m2_mt"), i + 1)
                    for h in range(KH):
                        last = mm(bank(5, 0, C), mst[:, h, :], wm_s[:, h, :], h == 0, h == KH - 1)
                    last.then_inc(sem("m2_wm"), 1)

                def m2_tn():
                    pe.wait_ge(sem("m2_1b"), i + 1)
                    pe.wait_ge(sem("m2_qt"), LEAD + i + 1)
                    turn(bank(4), mn[:, 2, :], "m2_tn")

                def m2_w1():
                    pe.wait_ge(sem("m2_nt"), LEAD + i + 1)
                    for o in range(4):
                        for h in range(4):
                            last = mm(bank(7, o * P, (o + 1) * P), w1_s[:, h, o * P:(o + 1) * P], cat[:, h, :],
                                      h == 0, h == 3)
                    last.then_inc(sem("m2_w1"), 1)

                def m2_w2():
                    pe.wait_ge(sem("m2_h"), LEAD + i + 1)
                    for h in range(4):
                        last = mm(bank(5, 0, C), ht[:, h, :], w2_s[:, h, :], h == 0, h == 3)
                    last.then_inc(sem("m2_w2"), 1)
                steps(i + TILES, {0: m2_turn, 2: m2_q, 5: m2_msg, 9: m2_tm, 11: m2_wm, 15: m2_tn, 16: m2_w1,
                                  18: m2_w2})
            pe.nop().then_inc(sem("main_over"), 1)

            pe.wait_ge(sem("main_over"), 4)
            pe.wait_ge(sem("ffw_in"), 16 * 8)

            def super_pe(i, tiles):
                n = tiles * P
                for j in range(tiles):
                    pe.wait_ge(sem(f"at_in{j}"), 32 * (i + 1))
                    pe.wait_ge(sem("b_r"), LEAD + i * SUP + (j - 1 if j >= 2 else 0))
                    agg = at_in[:, j, :, :, :].rearrange("p h g (n b) -> p h (g n) b", b=BASES)
                    for b in range(BASES):
                        for h in range(KH):
                            last = mm(bank(6 + j % 2, 0, C), agg[:, h, :, b], bases_s[:, b, h, :],
                                      b == 0 and h == 0, b == BASES - 1 and h == KH - 1)
                    last.then_inc(sem("b_mm"), 1)
                for j in range(tiles):
                    pe.wait_ge(sem("b_n"), i * SUP + j + 1)
                    pe.wait_ge(sem("b_xt"), LEAD + i * SUP + (j - 1 if j >= 2 else 0))
                    turn(bank(6 + j % 2, C, 2 * C), x1n[:, j, :], "b_tp")
                o0 = SUP * (EXPERTS + 1) * i
                pe.wait_ge(sem("b_xt"), LEAD + i * SUP + tiles)
                pe.wait_ge(sem("o_upd"), LEAD + o0)
                for j in range(tiles):
                    for h in range(KH):
                        last = mm(bank(5, j * EXPERTS, (j + 1) * EXPERTS), x1t[:, h, j * P:(j + 1) * P], wr_s[:, h, :],
                                  h == 0, h == KH - 1)
                last.then_inc(sem("r_lg"), 1)

                def layer(e, w, frm, b0, done):
                    for o in range(KH):
                        for h in range(KH):
                            last = mm(bank(b0 + o, 0, n), w[:, e, h, o * P:(o + 1) * P], frm[:, h, 0:n],
                                      h == 0, h == KH - 1)
                    last.then_inc(sem(done), 1)

                def first(e):
                    pe.wait_ge(sem("f_h1"), LEAD + KH * (EXPERTS * i + e))
                    layer(e, f1_s, x1t, 0, "f_l1")

                def second(e):
                    pe.wait_ge(sem("f_h1"), LEAD + KH * (EXPERTS * i + e + 1))
                    pe.wait_ge(sem("f_h2"), LEAD + KH * (EXPERTS * i + e))
                    layer(e, f2_s, h1, 2, "f_l2")

                def third(e):
                    pe.wait_ge(sem("f_h2"), LEAD + KH * (EXPERTS * i + e + 1))
                    pe.wait_ge(sem("o_upd"), LEAD + o0 + tiles * (e + 1))
                    for j in range(tiles):
                        for h in range(KH):
                            last = mm(bank(4 + j // 2, (j % 2) * C, (j % 2) * C + C), h2[:, h, j * P:(j + 1) * P],
                                      fo_s[:, e, h, :], h == 0, h == KH - 1)
                        last.then_inc(sem("f_l3"), 1)

                first(0)
                pe.wait_ge(sem("r_w"), i + 1)
                for j in range(tiles):
                    last = pe.transpose(bank(4, j * P, (j + 1) * P)[0:EXPERTS, :],
                                        rw[:, EXPERTS * j:EXPERTS * (j + 1)], ident[:, :])
                last.then_inc(sem("r_tp"), 1)
                pe.wait_ge(sem("r_wt"), i + 1)
                for j in range(tiles):
                    last = mm(bank(4 + j // 2, (j % 2) * C, (j % 2) * C + C), wt[:, j * P:(j + 1) * P], bo_s[:, :])
                last.then_inc(sem("f_bo"), 1)
                second(0)
                for e in range(1, EXPERTS):
                    first(e)
                    third(e - 1)
                    second(e)
                third(EXPERTS - 1)

            with pe.Fori(0, SUPERS) as i:
                super_pe(i, SUP)
            super_pe(SUPERS, 1)


_INS = ["x", "src", "dst", "edge_type_32", "edge_weight1", "L0_gnn_bases", "L0_gnn_w_comp", "L0_mix_Wq",
        "L0_mix_Wk", "L0_mix_Wv", "L0_mix_Wm", "L0_mix_W1", "L0_mix_W2", "L0_mix_g1", "L0_mix_b1", "L0_mix_g2",
        "L0_mix_b2", "L0_ffn_Wr", "L0_ffn_br", "L0_ffn_W1", "L0_ffn_b1", "L0_ffn_g1", "L0_ffn_be1", "L0_ffn_m1",
        "L0_ffn_v1", "L0_ffn_W2", "L0_ffn_b2", "L0_ffn_g2", "L0_ffn_be2", "L0_ffn_m2", "L0_ffn_v2", "L0_ffn_Wo",
        "L0_ffn_bo"]


def kernel(**inputs):
    import numpy as _np
    import concourse.bacc as _bacc
    from concourse import mybir as _mybir
    from concourse.bass_utils import run_bass_kernel_spmd as _run

    nc = _bacc.Bacc("TRN2", target_bir_lowering=False, num_devices=1)
    arrays, args = {}, []
    for name in _INS:
        a = _np.ascontiguousarray(inputs[name])
        arrays[f"in_{name}_dram"] = a
        args.append(nc.dram_tensor(f"in_{name}_dram", a.shape, _mybir.dt.from_np(a.dtype), kind="ExternalInput").ap())
    args.append(nc.dram_tensor("out_0_dram", (NODES, C), _mybir.dt.float32, kind="ExternalOutput").ap())
    gps_layer(nc, *args)
    r = _run(nc, [arrays], core_ids=[0])
    return r.results[0]["out_0_dram"]
```

```python
import concourse.bass as bass
from concourse import mybir
from contextlib import ExitStack

F32 = mybir.dt.float32
BF16 = mybir.dt.bfloat16
I32 = mybir.dt.int32
ALU = mybir.AluOpType
ACT = mybir.ActivationFunctionType
AX = mybir.AxisListType

P = 128
NODES, C = 6250, 256
EDGES = 200000
RELS, BASES = 32, 8
HEADS = 8
HD = C // HEADS
EXPERTS = 8
KH = C // P
TILES = -(-NODES // P)
LAST = NODES - (TILES - 1) * P
CHUNKS = -(-EDGES // P)
FULLC = EDGES // P
TAILE = EDGES - FULLC * P
CB = -(-CHUNKS // P)
CREST = CHUNKS - (CB - 1) * P

GN = P // BASES
GROUPS = -(-NODES // GN)
STEPS = CHUNKS + GROUPS - 1
UN = 20
ITERS = 2 * TILES
RING = 10
BATCH = 5
NB = UN // BATCH
SLOTS = 4
SB = 16
SPAD = SB * P
GPAD = 400
assert ITERS * UN >= STEPS and (ITERS + 2) * UN <= SPAD and ITERS * UN - CHUNKS < GPAD
assert UN % RING == 0 and UN % SLOTS == 0 and RING == 2 * BATCH

FAR = 8191
FAR_GROUP = FAR // GN
LN_EPS, ATT_EPS, BN_EPS = 1e-5, 1e-6, 1e-3
RSQRT_SEED = 0x5F3759DF
NEWTON = 3
NR1 = 2 + 3 * NEWTON
NRW = 2 + 4 * NEWTON

LG = 4
LT = (TILES - 1) // LG // 2
SUP = 4
SUPERS = (TILES - 1) // SUP
SORTK = 392


def gps_layer(nc, x, src, dst, etype, eweight, bases, w_comp, Wq, Wk, Wv, Wm, W1, W2, g1, b1, g2, b2,
              Wr, br, fW1, fb1, fg1, fbe1, fm1, fv1, fW2, fb2, fg2, fbe2, fm2, fv2, Wo, bo, out):
    ctx = ExitStack()
    with ctx:
        sems = {}

        def sem(name):
            if name not in sems:
                sems[name] = ctx.enter_context(nc.semaphore(name))
            return sems[name]

        def sb(name, shape, dt=F32):
            return ctx.enter_context(nc.sbuf_tensor(name, shape, dt))

        rec = nc.dram_tensor("edge_records", [CHUNKS, 4 * P], I32).ap()
        srt = nc.dram_tensor("sorted_edges", [CHUNKS * P, 4], I32).ap()
        cflat = nc.dram_tensor("step_chunks", [SPAD, 1], F32).ap()
        relS = nc.dram_tensor("step_types", [SPAD, P], F32).ap()
        xnD = nc.dram_tensor("normed_nodes", [(TILES + 1) * P, C], F32).ap()
        queryD = nc.dram_tensor("mix_queries", [(TILES + 1) * P, C], F32).ap()
        hiddenD = nc.dram_tensor("mix_hidden", [TILES * P, 2 * C], F32).ap()
        shiftD = nc.dram_tensor("mix_shifted", [TILES * P, C], F32).ap()
        baseD = nc.dram_tensor("mix_result", [(TILES + 1) * P, C], F32).ap()
        aggD = nc.dram_tensor("aggregates", [GPAD, P, C], F32).ap()

        ident = sb("ident", [P, P])
        ones = sb("ones", [P, P])
        iota16 = sb("iota16", [P, GN])
        relcol = sb("relcol", [P, 1])
        chunk_no = sb("chunk_no", [P, CB])
        step_no = sb("step_no", [P, SB])
        wblk = sb("wblk", [P, 4 * BASES])
        kvmask = sb("kvmask", [P, P])
        headmask = sb("headmask", [P, 4])
        rowmask = sb("rowmask", [P, TILES])
        wq_s = sb("wq_s", [P, KH, C])
        wkv_s = sb("wkv_s", [P, KH, 2 * C])
        wm_s = sb("wm_s", [P, KH, C])
        w1_s = sb("w1_s", [P, 4, 2 * C])
        w2_s = sb("w2_s", [P, 4, C])
        lnw = sb("lnw", [P, 2, C])
        wr_s = sb("wr_s", [P, KH, EXPERTS])
        br_s = sb("br_s", [P, EXPERTS])
        bo_s = sb("bo_s", [EXPERTS, C])
        bases_s = sb("bases_s", [P, BASES, KH, C])
        ffw = sb("ffw", [P, 3 * EXPERTS * KH * C])
        f1_s, f2_s, fo_s = (ffw[:, n * EXPERTS * KH * C:(n + 1) * EXPERTS * KH * C].rearrange(
            "p (e k n) -> p e k n", e=EXPERTS, k=KH) for n in range(3))
        bnc = sb("bnc", [P, 4, 2 * EXPERTS])

        def carver(name, words):
            t = sb(name, [P, words])
            place = [0]

            def carve(n, at=None):
                a = place[0] if at is None else at
                place[0] = max(place[0], a + n)
                assert place[0] <= words, (name, place[0])
                return t[:, a:a + n]
            return carve

        ARENA = 20480
        carve = carver("arena", ARENA)
        ring = carve(RING * C).rearrange("p (r n) -> p r n", r=RING)
        acc = carve(RING * C).rearrange("p (r n) -> p r n", r=RING)
        selm = carve(2 * BATCH * P).rearrange("p (u s n b) -> p u s n b", u=2, s=BATCH, b=BASES)
        relb = carve(BATCH * P).rearrange("p (j e) -> p j e", j=BATCH)
        relhot = carve(BATCH * P).rearrange("p (j e) -> p j e", j=BATCH)
        table = carve(3 * SPAD).rearrange("p (f s) -> p f s", f=3)
        keep = carve(SPAD)
        rowsI = carve(SPAD).bitcast(I32)
        grow = rowsI[0:1, :]
        hot = carve(UN * GN).rearrange("p (s n) -> p s n", s=UN)
        coef = carve(UN * BASES).rearrange("p (s b) -> p s b", s=UN)
        keepc = carve(UN)
        idxc = carve(UN).bitcast(I32)
        irec = carve(4 * 4 * P, 0).bitcast(I32).rearrange("p (u n) -> p u n", u=4)
        ifld = carve(4 * 3 * P, RING * C).rearrange("p (u f n) -> p u f n", u=4, f=3)
        junk = carve(CB * P // 2, RING * C + 4 * 3 * P).bitcast(BF16)
        crow = carve(SPAD + 1, 2 * RING * C)
        chk_a = carve(EDGES // 125, 0)[0:125, :].bitcast(I32)
        chk_b = carve(EDGES // 125, RING * C)[0:125, :].bitcast(I32)
        chk_c = carve(EDGES // 125, 2 * RING * C + 2 * BATCH * P + 2 * BATCH * P)[0:125, :]
        CHKP, CHKN = 125, EDGES // 125

        def tiled(at):
            return carve(SUP * C, at).rearrange("p (j n) -> p j n", j=SUP)

        at_in = carve(SUP * 8 * C, 0).rearrange("p (j h g n) -> p j h g n", j=SUP, h=KH, g=8)
        base_in, x_in, xr, x1, x1n, oacc = (tiled((8 + n) * SUP * C) for n in range(6))
        x1t, h1, h2 = (carve(KH * SUP * P, (14 + n) * SUP * C).rearrange("p (k n) -> p k n", k=KH) for n in range(3))
        rest = 17 * SUP * C
        lg, ex, rw = (carve(SUP * EXPERTS, rest + n * SUP * EXPERTS) for n in range(3))
        rmx, rsm, rin = (carve(SUP, rest + 3 * SUP * EXPERTS + n * SUP) for n in range(3))
        bst = carve(SUP * 6, rest + 4 * SUP * EXPERTS).rearrange("p (j n) -> p j n", j=SUP)
        bmv = carve(SUP * 2, rest + 5 * SUP * EXPERTS).rearrange("p (j n) -> p j n", j=SUP)
        wt = carve(SUP * P, rest + 6 * SUP * EXPERTS)[0:EXPERTS, :]

        lns = sb("lns", [P, LT, 6])
        lnmv = sb("lnmv", [P, LT, 2])
        nrw = sb("nrw", [P, 4, 2 * P])
        nri = sb("nri", [P, 2 * P], I32)
        cstep = sb("cstep", [P, SB])
        cint = sb("cint", [P, SB + 4], I32)
        gbase = sb("gbase", [P, 2, SB + 4])
        colc = sb("colc", [P, 4], I32)
        colg = sb("colg", [P, 4])
        fdst = sb("fdst", [P, CB], I32)
        fgrp = sb("fgrp", [P, CB], I32)
        tcol = sb("tcol", [P, CB])
        diag = sb("diag", [P, 2, P])
        PADE = P - TAILE
        padc = sb("padc", [1, 4 * PADE], I32)
        zrow = sb("zrow", [P, KH * (P + 1)])
        flag = sb("flag", [1, 1], I32)
        flagf = sb("flagf", [P, 1])
        mix = carver("mixbuf", 20 * C)
        xt, shifted, ek, rk, eq, rq, ksb, msb, n1, mo = (mix(C) for _ in range(10))
        mo2 = ksb
        xnt, mst, qt, nt = (mix(C).rearrange("p (k n) -> p k n", k=KH) for _ in range(4))
        hpart, hsum, ht = (mix(2 * C).rearrange("p (k n) -> p k n", k=4) for _ in range(3))
        vx = sb("vx", [P, KH, P + 1])
        kvb = sb("kvb", [P, KH, P + 4])
        zt = sb("zt", [P, HEADS])
        zi = sb("zi", [P, HEADS])
        gb1 = sb("gb1", [P, 2, KH])
        lst = sb("lst", [P, 2, 6])
        lmv = sb("lmv", [P, 2, 2])
        lnr = sb("lnr", [P, 4, 2])
        lnu = sb("lnu", [P, 2, 2])
        shift1 = sb("shift1", [P, 1])
        lnx = mix(2 * LT * C, 0).rearrange("p (h t n) -> p h t n", h=2, t=LT)
        bnrow = mix(10 * P, 2 * LT * C)[0:2 * EXPERTS, :].rearrange("p (v n) -> p v n", v=10)
        bnt = mix(4 * P, 2 * LT * C + 10 * P)[0:2 * EXPERTS, :].rearrange("p (v n) -> p v n", v=4)
        bnd = mix(2 * P, 2 * LT * C + 14 * P)[0:2 * EXPERTS, :].rearrange("p (l n) -> p l n", l=2)

        PS = ctx.enter_context(nc.psum_tensor("PS", [P, 8 * 512], F32))

        QN = UN * BASES

        def bank(n, a=0, b=512):
            return PS[:, n * 512 + a:n * 512 + b]

        so = [0]

        def carve_s(words):
            at = so[0]
            so[0] += words
            assert so[0] <= 3 * EXPERTS * KH * C
            return ffw[:, at:at + words]

        s_dst = carve_s(CHUNKS).bitcast(I32)
        s_oth = carve_s(3 * CHUNKS).rearrange("p (f n) -> p f n", f=3).bitcast(I32)
        s_key = carve_s(CHUNKS)
        s_rank = carve_s(CHUNKS)
        s_iota = carve_s(SORTK)
        s_run = carve_s(SORTK)
        s_start = carve_s(SORTK)
        s_tmp = carve_s(SORTK)
        s_one = carve_s(SORTK // 2).bitcast(BF16)
        s_low = carve_s(P // 2).bitcast(BF16)
        s_all = carve_s(P // 2).bitcast(BF16)
        s_col = carve_s(2)
        s_idx = carve_s(1).bitcast(I32)
        s_rec = carve_s(4).bitcast(I32)
        s_blk = bases_s[:, :, :, :].rearrange("p a b n -> p (a b n)")[:, 0:8 * P].bitcast(I32).rearrange(
            "p (h n) -> p h n", h=2)

        def wait_apart(eng, name, value):
            eng.wait_ge(sem(name), value)
            eng.sem_inc(sem("passed"), 1)

        LEAD, DLEAD = 1, 16
        LED = {
            "pe": ("m1_kv", "m1_acc", "m1_w1", "m2_w1", "m2_wm", "m2_w2", "m2_tm", "m2_tn", "m2_msg", "coef_mm", "fld_tp",
                   "f_l1", "f_l2", "f_l3", "b_mm", "b_tp"),
            "dve": ("m1_k", "m1_q", "m1_plus", "m2_sum", "m2_base", "coef_ready", "sel_ready", "b_x", "b_r", "o_upd"),
            "act": ("m1_xt", "m1_v", "m1_hid", "m1_qparts", "m2_n1", "m2_h", "table_cp", "b_xt", "f_h1", "f_h2"),
        }

        def start_ahead(eng, who):
            for name in LED[who]:
                eng.sem_inc(sem(name), LEAD)

        LED_DMA = ["ln_st0", "ln_st1", "base_out", "out_st", "query_out", "hidden_out",
                   "shift_out"] + [f"rels_out{u}" for u in range(4)] + \
                  [f"flush{r}" for r in range(RING)]
        lead_s = sb("lead_s", [1, 4 * (len(LED_DMA) + 1)])

        def dma_ahead(eng, name, n):
            eng.dma_start(lead_s[:, 4 * n:4 * n + 4], x[0:1, 0:4]).then_inc(sem(name), DLEAD)

        class Chain:

            def __init__(self, eng, name):
                self.eng, self.name, self.n = eng, name, 0

            def put(self, ins):
                self.n = self.n + 1
                ins.then_inc(sem(self.name), 1)

            def need(self):
                self.eng.wait_ge(sem(self.name), self.n)

            def __call__(self, ins, apart=False):
                self.n = self.n + 1
                ins.then_inc(sem(self.name), 1)
                if apart:
                    wait_apart(self.eng, self.name, self.n)
                else:
                    self.eng.wait_ge(sem(self.name), self.n)

        block = ctx.enter_context(nc.Block())
        def rows(ap, k):
            return ap.rearrange("(k p) n -> p k n", p=P)

        @block.sync
        def _(sp):
            sp.dma_start(chk_a, dst.rearrange("(p n) -> p n", p=CHKP)).then_inc(sem("chk_in"), 16)
            sp.wait_ge(sem("dve_const"), 2)
            sp.dma_start(chk_b[0:CHKP - 1, :],
                         dst[1:1 + (CHKP - 1) * CHKN].rearrange("(p n) -> p n", n=CHKN)).then_inc(sem("chk_in"), 16)
            sp.dma_start(chk_b[CHKP - 1:CHKP, 0:CHKN - 1],
                         dst[1 + (CHKP - 1) * CHKN:EDGES].rearrange("(p n) -> p n", p=1)).then_inc(sem("chk_in"), 16)

            def load_nodes(i, h):
                sp.dma_start(lnx[:, h, :, :], x[bass.ds(i * (2 * LT * P) + h * LT * P, LT * P), :].rearrange(
                    "(t p) n -> p t n", p=P)).then_inc(sem(f"ln_ld{h}"), 16)

            for h in range(2):
                load_nodes(0, h)
            for n in range(2):
                dma_ahead(sp, LED_DMA[n], n)
            fields = [src, dst, etype, eweight.rearrange("e a -> (e a)").bitcast(I32)]
            for f, v in enumerate(fields):
                sp.dma_start(rec[0:FULLC, f * P:(f + 1) * P],
                             v[0:FULLC * P].rearrange("(c e) -> c e", e=P)).then_inc(sem("rec_in"), 16)
                sp.dma_start(rec[FULLC:CHUNKS, f * P:f * P + TAILE],
                             v[FULLC * P:EDGES].rearrange("(a e) -> a e", a=1)).then_inc(sem("rec_in"), 16)
            sp.wait_ge(sem("dve_const"), 5)
            sp.dma_start(rec[FULLC:CHUNKS, :].rearrange("a (f e) -> a f e", f=4)[:, :, TAILE:P],
                         padc[:, :].rearrange("a (f e) -> a f e", f=4)).then_inc(sem("rec_in"), 16)
            sp.wait_ge(sem("dve_const"), 6)
            sp.dma_start(xnD[TILES * P:(TILES + 1) * P, :], zrow[:, 0:C]).then_inc(sem("xn_out"), 16)
            sp.dma_start(queryD[TILES * P:(TILES + 1) * P, :], zrow[:, 0:C]).then_inc(sem("xn_out"), 16)
            with sp.Fori(1, LG) as i:
                for h in range(2):
                    sp.wait_ge(sem(f"ln_st{h}"), DLEAD + 16 * i)
                    load_nodes(i, h)
            for n in range(2, len(LED_DMA)):
                dma_ahead(sp, LED_DMA[n], n)
            sp.wait_ge(sem("ln_st0"), DLEAD + 16 * LG)
            sp.wait_ge(sem("ln_zero"), 1)
            sp.dma_start(lnx[0:LAST, 0, 0, :], x[(TILES - 1) * P:NODES, :]).then_inc(sem("ln_ld0"), 16)

            sp.wait_ge(sem("flag_ready"), 1)
            unsorted = sp.value_load(flag[0:1, 0:1], min_val=0, max_val=1)
            with sp.If(unsorted > 0):
                sp.wait_ge(sem("s_fill"), 2)
                sp.wait_ge(sem("rec_in"), 16 * 9)
                lane = (P - 1) * CHUNKS
                for n, (t, v) in enumerate(((s_dst, dst), (s_oth[:, 0, :], src), (s_oth[:, 1, :], etype),
                                            (s_oth[:, 2, :], fields[3]))):
                    sp.dma_start(t[0:P - 1, :], v[0:lane].rearrange("(p n) -> p n", n=CHUNKS)
                                 ).then_inc(sem("s_in"), 16)
                    sp.dma_start(t[P - 1:P, 0:EDGES - lane], v[lane:EDGES].rearrange("(a n) -> a n", a=1)
                                 ).then_inc(sem("s_in"), 16)
                sp.wait_ge(sem("s_scat"), DLEAD + 16 * CHUNKS)
                for j in range(CB):
                    n = P if j < CB - 1 else CREST
                    if j:
                        sp.wait_ge(sem("s_rout"), 16 * j)
                    sp.dma_start(s_blk[0:n, 0, :], srt[j * P * P:j * P * P + n * P, :].rearrange(
                        "(c e) f -> c (e f)", e=P)).then_inc(sem("s_rin"), 16)
                    sp.wait_ge(sem("s_turn"), 2 * j + 2)
                    sp.dma_start(rec[j * P:j * P + n, :], s_blk[0:n, 1, :]).then_inc(sem("s_rout"), 16)
                sp.wait_ge(sem("s_rout"), 16 * CB)
            sp.wait_ge(sem("rec_in"), 16 * 9)
            sp.sem_inc(sem("rec_ready"), 1)

            with nc.allow_non_contiguous_dma(reason="one word per chunk"):
                sp.wait_ge(sem("dve_const"), 7)
                sp.dma_start(fdst[:, 0:CB - 1], rec[0:(CB - 1) * P, P:P + 1].rearrange(
                    "(j p) a -> p (j a)", p=P), allow_slow_non_contiguous=True).then_inc(sem("fdst_in"), 16)
                sp.dma_start(fdst[0:CREST, CB - 1:CB], rec[(CB - 1) * P:CHUNKS, P:P + 1]
                             ).then_inc(sem("fdst_in"), 16)
                sp.wait_ge(sem("cstep_ready"), SB)
                sp.dma_start(cflat.rearrange("(j p) a -> p (j a)", p=P), cstep[:, :],
                             allow_slow_non_contiguous=True).then_inc(sem("cflat_out"), 16)
            sp.wait_ge(sem("cflat_out"), 16)
            sp.dma_start(crow[:, 1:SPAD + 1], cflat.rearrange("s a -> a s").to_broadcast([P, SPAD])
                         ).then_inc(sem("crow_in"), 16)
            with sp.Fori(0, SB // 4) as i:
                for u in range(4):
                    sp.wait_ge(sem("fld_type"), 4 * i + u + 1)
                    sp.dma_start(relS[bass.ds((4 * i + u) * P, P), :], ifld[:, u, 2, :]
                                 ).then_inc(sem(f"rels_out{u}"), 16)
            for u in range(4):
                sp.wait_ge(sem(f"rels_out{u}"), DLEAD + 16 * (SB // 4))

            def load_types(it):
                v = relS.rearrange("(j q) e -> q j e", q=4)
                for q in range(4):
                    s = v[q:q + 1, bass.ds(it * BATCH, BATCH), :]
                    sp.dma_start(relb[32 * q:32 * q + 32, :, :], s.to_broadcast([32, BATCH, P])
                                 ).then_inc(sem("types_in"), 16)

            load_types(0)
            sp.wait_ge(sem("relhot_ready"), 1)
            load_types(1)
            sp.wait_ge(sem("xn_out"), 32)
            sp.wait_ge(sem("ln_st0"), DLEAD + 16 * (LG + 1))
            sp.wait_ge(sem("ln_st1"), DLEAD + 16 * LG)
            sp.sem_inc(sem("xn_ready"), 1)
            sp.dma_start(xt[:, :], xnD[0:P, :]).then_inc(sem("xt_in"), 16)
            sp.wait_ge(sem("tables_ready"), 2)

            gregs = [sp.alloc_register(f"group{k}") for k in range(UN + 1)]

            def steps(it, extra):
                sp.load(gregs, grow[:, bass.ds(it * UN, UN + 1)])
                g = [sp.snap(r, min_val=0, max_val=GPAD - 1) for r in gregs]
                for k in range(UN):
                    s = it * UN + k
                    if k in extra:
                        extra[k]()
                    sp.wait_ge(sem("acc_done"), s + 1 + SLOTS)
                    sp.dma_start(aggD[bass.ds(g[k], 1), :, :].rearrange("a p n -> p (a n)"), acc[:, k % RING, :],
                                 cond=(g[k + 1] > g[k])).then_inc(sem(f"flush{k % RING}"), 16)

            def next_types(it):
                sp.wait_ge(sem("relhot_ready"), it + 2)
                load_types(it + 2)

            with sp.Fori(0, TILES) as i:
                def next_x():
                    wait_apart(sp, "m1_tp", i + 1)
                    sp.wait_ge(sem("m1_plus"), LEAD + i + 1)
                    sp.dma_start(xt[:, :], xnD[bass.ds((i + 1) * P, P), :]).then_inc(sem("xt_in"), 16)
                steps(i, {5: next_x, 12: lambda: next_types(i)})
            for name in ("query_out", "hidden_out", "shift_out"):
                sp.wait_ge(sem(name), DLEAD + 16 * TILES)
            sp.dma_start(qt[:, :, :].rearrange("p k n -> p (k n)"), queryD[0:P, :]).then_inc(sem("query_in"), 16)
            sp.dma_start(hpart[:, :, :].rearrange("p k n -> p (k n)"), hiddenD[0:P, :]).then_inc(sem("hidden_in"), 16)
            sp.dma_start(shifted[:, :], shiftD[0:P, :]).then_inc(sem("shift_in"), 16)
            with sp.Fori(0, TILES) as i:
                def next_query():
                    wait_apart(sp, "m2_msg", LEAD + i + 1)
                    sp.dma_start(qt[:, :, :].rearrange("p k n -> p (k n)"), queryD[bass.ds((i + 1) * P, P), :]
                                 ).then_inc(sem("query_in"), 16)

                def next_hidden():
                    wait_apart(sp, "m2_sum", LEAD + i + 1)
                    sp.dma_start(hpart[:, :, :].rearrange("p k n -> p (k n)"), hiddenD[bass.ds(i * P, P), :]
                                 ).then_inc(sem("hidden_in"), 16)

                def next_shift():
                    wait_apart(sp, "m2_base", LEAD + i + 1)
                    sp.dma_start(shifted[:, :], shiftD[bass.ds(i * P, P), :]).then_inc(sem("shift_in"), 16)
                steps(i + TILES, {4: next_query, 10: next_hidden, 12: lambda: next_types(i + TILES), 18: next_shift})
            sp.wait_ge(sem("xt_in"), 16 * (TILES + 1))
            sp.wait_ge(sem("query_in"), 16 * (TILES + 1))
            sp.wait_ge(sem("types_in"), 64 * (ITERS + 2))
            for r in range(RING):
                sp.wait_ge(sem(f"flush{r}"), DLEAD + 16 * ITERS * UN // RING)
            sp.wait_ge(sem("base_out"), DLEAD + 16 * (TILES + 1))
            sp.wait_ge(sem("main_over"), 4)

            def load_super(i, tiles, n):
                for j in range(tiles):
                    t = i * SUP + j
                    sp.wait_ge(sem("b_mm"), LEAD + i * SUP)
                    for h in range(KH):
                        sp.dma_start(at_in[:, j, h, :, :], aggD[bass.ds(t * 8, 8), :, h * P:(h + 1) * P].rearrange(
                            "g p n -> p g n")).then_inc(sem(f"at_in{j}"), 16)
                sp.wait_ge(sem("b_x"), LEAD + i * SUP)
                if tiles == SUP:
                    sp.dma_start(base_in[:, :, :], baseD[bass.ds(i * (SUP * P) + P, SUP * P), :].rearrange(
                        "(j p) n -> p j n", p=P)).then_inc(sem("bx_in"), 16)
                    sp.dma_start(x_in[:, :, :], x[bass.ds(i * (SUP * P), SUP * P), :].rearrange(
                        "(j p) n -> p j n", p=P)).then_inc(sem("bx_in"), 16)
                else:
                    sp.dma_start(base_in[:, 0, :], baseD[TILES * P:(TILES + 1) * P, :]).then_inc(sem("bx_in"), 16)
                    sp.wait_ge(sem("x_zero"), 1)
                    sp.dma_start(x_in[0:LAST, 0, :], x[(TILES - 1) * P:NODES, :]).then_inc(sem("bx_in"), 16)

            with sp.Fori(0, SUPERS) as i:
                load_super(i, SUP, P)
            load_super(SUPERS, 1, LAST)
            sp.wait_ge(sem("out_st"), DLEAD + 16 * (SUPERS + 1))

        @block.gpsimd
        def _(pool):
            dma_ahead(pool, "s_scat", len(LED_DMA))
            const = Chain(pool, "pool_const")

            def iota(o, pattern, cm=0):
                const(pool.iota(o, pattern, base=0, channel_multiplier=cm, allow_small_or_imprecise_dtypes=True))

            iota(iota16[:, :], [[1, GN]])
            iota(grow, [[1, SPAD]])
            iota(chunk_no[:, :], [[P, CB]], 1)
            iota(step_no[:, :], [[P, SB]], 1)
            for q in range(4):
                iota(relcol[32 * q:32 * q + 32, :], [[0, 1]], 1)
            pool.wait_ge(sem("dve_const"), 1)
            const(pool.affine_select(out=ident[:, :], in_=ident[:, :], compare_op=ALU.not_equal, fill=1.0, base=0,
                                     pattern=[[-1, P]], channel_multiplier=1))
            pool.wait_ge(sem("dve_const"), 8)
            const(pool.affine_select(out=rowmask[:, :], in_=rowmask[:, :], compare_op=ALU.is_gt, fill=0.0, base=NODES,
                                     pattern=[[-P, TILES]], channel_multiplier=-1))

            pool.wait_ge(sem("flag_ready"), 1)
            unsorted = pool.value_load(flag[0:1, 0:1], min_val=0, max_val=1)
            with pool.If(unsorted > 0):
                pool.iota(s_iota, [[1, SORTK]], base=0, channel_multiplier=0,
                          allow_small_or_imprecise_dtypes=True).then_inc(sem("s_const"), 1)
                pool.wait_ge(sem("s_lowone"), 1)
                pool.affine_select(out=s_low, in_=s_low, compare_op=ALU.is_gt, fill=0.0, base=0,
                                   pattern=[[1, P]], channel_multiplier=-1).then_inc(sem("s_const"), 1)
                with pool.Fori(0, CHUNKS) as i:
                    wait_apart(pool, "s_recs", i + 1)
                    pool.indirect_dma_start(out=srt, out_offset=bass.IndirectOffsetOnAxis(ap=s_idx, axis=0),
                                            in_=s_rec, in_offset=None).then_inc(sem("s_scat"), 16)

            pool.wait_ge(sem("rec_ready"), 1)
            with pool.Fori(0, SB // 4) as i:
                for u in range(4):
                    wait_apart(pool, "col_ready", i * 4 + u + 1)
                    pool.indirect_dma_start(out=irec[:, u, :], out_offset=None, in_=rec,
                                            in_offset=bass.IndirectOffsetOnAxis(ap=colc[:, u:u + 1], axis=0)
                                            ).then_inc(sem(f"irec_in{u}"), 16)
            pool.wait_ge(sem("xn_ready"), 1)

            def steps(it):
                for k in range(UN):
                    if k % RING == 0:
                        pool.wait_ge(sem("idx_ready"), 2 * it + k // RING + 1)
                    wait_apart(pool, "mm_done", it * UN + k + 1)
                    pool.indirect_dma_start(out=ring[:, k % RING, :], out_offset=None, in_=xnD,
                                            in_offset=bass.IndirectOffsetOnAxis(ap=idxc[:, k:k + 1], axis=0)
                                            ).then_inc(sem(f"row_in{k % RING}"), 16)

            with pool.Fori(0, ITERS) as it:
                steps(it)
            pool.nop().then_inc(sem("main_over"), 1)

        @block.scalar
        def _(act):
            start_ahead(act, "act")
            for q in range(4):
                act.wait_ge(sem("dve_const"), 3)
                act.dma_start(wblk[32 * q:32 * q + 32, BASES * q:BASES * (q + 1)], w_comp).then_inc(sem("w_in"), 16)
            act.dma_start(wq_s[:, :, :], rows(Wq, KH)).then_inc(sem("w_in"), 16)
            act.dma_start(wkv_s[:, :, 0:C], rows(Wk, KH)).then_inc(sem("w_in"), 16)
            act.dma_start(wkv_s[:, :, C:2 * C], rows(Wv, KH)).then_inc(sem("w_in"), 16)
            act.dma_start(wm_s[:, :, :], rows(Wm, KH)).then_inc(sem("w_in"), 16)
            act.dma_start(w1_s[:, :, :], rows(W1, 4)).then_inc(sem("w_in"), 16)
            act.dma_start(w2_s[:, :, :], rows(W2, 4)).then_inc(sem("w_in"), 16)
            with nc.allow_non_contiguous_dma(reason="one word per feature"):
                for n, v in enumerate((g1, b1)):
                    act.dma_start(gb1[:, n, :], v.rearrange("(k p) -> p k", p=P), allow_slow_non_contiguous=True
                                  ).then_inc(sem("w_in"), 16)
            for n, v in enumerate((g2, b2)):
                act.dma_start(lnw[:, n, :], v.rearrange("(a n) -> a n", a=1).to_broadcast([P, C])
                              ).then_inc(sem("w_in"), 16)
            act.dma_start(wr_s[:, :, :], rows(Wr, KH)).then_inc(sem("w_in"), 16)
            act.dma_start(br_s[:, :], br.rearrange("(a n) -> a n", a=1).to_broadcast([P, EXPERTS])
                          ).then_inc(sem("w_in"), 16)
            act.dma_start(bo_s[:, :], bo).then_inc(sem("w_in"), 16)
            for n, v in enumerate((fb1, fg1, fbe1, fm1, fv1, fb2, fg2, fbe2, fm2, fv2)):
                act.dma_start(bnrow[:, n, :], v.rearrange("e (k p) -> (e k) p", p=P)).then_inc(sem("bn_in"), 16)

            with act.Fori(0, LG) as i:
                for h in range(2):
                    at = i * (2 * LT * P) + h * LT * P
                    act.wait_ge(sem(f"ln_n{h}"), LT * (i + 1))
                    act.dma_start(xnD[bass.ds(at, LT * P), :].rearrange("(t p) n -> p t n", p=P), lnx[:, h, :, :]
                                  ).then_inc(sem(f"ln_st{h}"), 16)
            act.wait_ge(sem("ln_n0"), LT * LG + 1)
            act.dma_start(xnD[(TILES - 1) * P:TILES * P, :], lnx[:, 0, 0, :]).then_inc(sem("ln_st0"), 16)

            act.wait_ge(sem("rec_ready"), 1)
            for t, w in ((f1_s, fW1), (f2_s, fW2), (fo_s, Wo)):
                for k in range(KH):
                    act.dma_start(t[:, :, k, :], w[:, k * P:(k + 1) * P, :].rearrange("e p n -> p e n")
                                  ).then_inc(sem("ffw_in"), 16)
            for k in range(KH):
                act.dma_start(bases_s[:, :, k, :], bases[:, k * P:(k + 1) * P, :].rearrange("b p n -> p b n")
                              ).then_inc(sem("ffw_in"), 16)

            act.wait_ge(sem("bn_tp"), 1)
            act.copy(bnc[:, :, :].rearrange("p a e -> p (a e)"), bank(3, 0, 8 * EXPERTS)).then_inc(sem("bnc_ready"), 1)

            with act.Fori(0, SB // 4) as i:
                for u in range(4):
                    act.wait_ge(sem("fld_tp"), LEAD + 4 * i + u + 1)
                    act.copy(table[:, :, bass.ds((4 * i + u) * P, P)],
                             bank(u % 2, 0, 3 * P).rearrange("p (f e) -> p f e", f=3)).then_inc(sem("table_cp"), 1)

            with act.Fori(0, TILES) as i:
                act.wait_ge(sem("m1_tp"), i + 1)
                act.wait_ge(sem("m1_w1"), LEAD + i)
                act.copy(xnt[:, :, :].rearrange("p k n -> p (k n)"), bank(4, 0, C)).then_inc(sem("m1_xt"), 1)
                act.wait_ge(sem("m1_kv"), LEAD + i + 1)
                act.wait_ge(sem("m1_k"), LEAD + i)
                act.activation(ek[:, :], bank(5, 0, C), ACT.Exp).then_inc(sem("m1_parts"), 1)
                act.activation(rk[:, :], bank(5, 0, C), ACT.Relu).then_inc(sem("m1_parts"), 1)
                act.wait_ge(sem("m1_acc"), LEAD + i)
                act.activation(vx[:, :, 0:P], bank(5, C, 2 * C).rearrange("p (k n) -> p k n", k=KH), ACT.Copy,
                               scale=1.0 / NODES).then_inc(sem("m1_v"), 1)
                act.copy(vx[:, :, P:P + 1], rowmask[:, bass.ds(i, 1)].unsqueeze(1).to_broadcast([P, KH, 1])
                         ).then_inc(sem("m1_v"), 1)
                act.wait_ge(sem("m1_query"), i + 1)
                act.wait_ge(sem("m1_q"), LEAD + i)
                act.activation(eq[:, :], bank(4, C, 2 * C), ACT.Exp).then_inc(sem("m1_qparts"), 1)
                act.activation(rq[:, :], bank(4, C, 2 * C), ACT.Relu).then_inc(sem("m1_qparts"), 1)
                act.wait_ge(sem("m1_plus"), LEAD + i + 1)
                act.dma_start(shiftD[bass.ds(i * P, P), :], shifted[:, :]).then_inc(sem("shift_out"), 16)
                act.wait_ge(sem("m1_q"), LEAD + i + 1)
                act.dma_start(queryD[bass.ds(i * P, P), :], qt[:, :, :].rearrange("p k n -> p (k n)")
                              ).then_inc(sem("query_out"), 16)
                act.wait_ge(sem("m1_w1"), LEAD + i + 1)
                act.wait_ge(sem("hidden_out"), DLEAD + 16 * i)
                act.copy(hpart[:, :, :].rearrange("p k n -> p (k n)"), bank(5)).then_inc(sem("m1_hid"), 1)
                act.wait_ge(sem("m1_hid"), LEAD + i + 1)
                act.dma_start(hiddenD[bass.ds(i * P, P), :], hpart[:, :, :].rearrange("p k n -> p (k n)")
                              ).then_inc(sem("hidden_out"), 16)
            act.copy(n1[:, 0:P], ones[:, :]).then_inc(sem("n1_fill"), 1)
            act.copy(n1[:, P:C], ones[:, :]).then_inc(sem("n1_fill"), 1)
            act.activation(lnr[:, 1, 0:2], ones[:, 0:2], ACT.Sqrt).then_inc(sem("root_table"), 1)
            act.wait_ge(sem("root_table"), 1)

            def root(i, a):
                act.wait_ge(sem("ln_var"), i + 1)
                act.activation(lnr[:, 1, a:2], lnr[:, 0, a:2], ACT.Sqrt).then_inc(sem("ln_root"), 1)

            def act_hidden(i):
                act.wait_ge(sem("m2_tn"), LEAD + i + 1)
                for k in range(KH):
                    act.activation(nt[:, k, :], bank(4, k * P, (k + 1) * P), ACT.Identity, bias=gb1[:, 1, k:k + 1],
                                   scale=gb1[:, 0, k:k + 1]).then_inc(sem("m2_nt"), 1)
                act.wait_ge(sem("m2_sum"), LEAD + i + 1)
                act.wait_ge(sem("m2_w2"), LEAD + i)
                act.activation(ht[:, :, :].rearrange("p k n -> p (k n)"),
                               hsum[:, :, :].rearrange("p k n -> p (k n)"), ACT.Relu).then_inc(sem("m2_h"), 1)

            def store_base(i):
                act.wait_ge(sem("m2_base"), LEAD + i + 1)
                act.dma_start(baseD[bass.ds(i * P, P), :], mo[:, :]).then_inc(sem("base_out"), 16)

            with act.Fori(0, TILES) as i:
                act_hidden(i)
                act.wait_ge(sem("m2_tm"), LEAD + i + 1)
                act.wait_ge(sem("m2_wm"), LEAD + i)
                act.copy(mst[:, :, :].rearrange("p k n -> p (k n)"), bank(4, 0, C)).then_inc(sem("m2_mt"), 1)
                root(i, 0)
                act.wait_ge(sem("ln_scale"), i + 1)
                act.activation(n1[:, :], bank(5, 0, C), ACT.Identity, bias=shift1[:, 0:1], scale=lnu[:, 1, 0:1]
                               ).then_inc(sem("m2_n1"), 1)
                store_base(i)
            act_hidden(TILES)
            root(TILES, 1)
            store_base(TILES)
            act.nop().then_inc(sem("main_over"), 1)

            def take_turned(i, tiles):
                for j in range(tiles):
                    act.wait_ge(sem("b_tp"), LEAD + i * SUP + j + 1)
                    if j == 0:
                        act.wait_ge(sem("f_l1"), LEAD + EXPERTS * i)
                    act.copy(x1t[:, :, j * P:(j + 1) * P], bank(6 + j % 2, C, 2 * C).rearrange(
                        "p (k n) -> p k n", k=KH)).then_inc(sem("b_xt"), 1)

            def router_exp(i, tiles):
                act.wait_ge(sem("r_sub"), i + 1)
                act.activation(ex[:, 0:tiles * EXPERTS], lg[:, 0:tiles * EXPERTS], ACT.Exp).then_inc(sem("r_exp"), 1)

            def feed(i, tiles, nxt, ntiles):
                n = tiles * P

                def hidden(e, layer):
                    o, b0, s = ((h1, 0, "1"), (h2, 2, "2"))[layer]
                    act.wait_ge(sem(f"f_l{s}"), LEAD + EXPERTS * i + e + 1)
                    if layer == 0:
                        act.wait_ge(sem("f_l2"), LEAD + EXPERTS * i + e)
                    else:
                        act.wait_ge(sem("f_l3"), LEAD + SUP * EXPERTS * i + tiles * e)
                    for k in range(KH):
                        act.activation(o[:, k, 0:n], bank(b0 + k, 0, n), ACT.Relu,
                                       bias=bnc[:, 2 * layer + 1, 2 * e + k:2 * e + k + 1],
                                       scale=bnc[:, 2 * layer, 2 * e + k:2 * e + k + 1]).then_inc(sem(f"f_h{s}"), 1)

                hidden(0, 0)
                act.wait_ge(sem("r_tp"), i + 1)
                act.copy(wt[:, 0:n], bank(4, 0, n)[0:EXPERTS, :]).then_inc(sem("r_wt"), 1)
                hidden(0, 1)
                for e in range(1, EXPERTS):
                    hidden(e, 0)
                    if e == EXPERTS - 1:
                        take_turned(nxt, ntiles)
                    hidden(e, 1)
                if ntiles:
                    router_exp(nxt, ntiles)
                act.wait_ge(sem("o_upd"), LEAD + SUP * (EXPERTS + 1) * i + tiles * (EXPERTS + 1))
                if tiles == SUP:
                    act.dma_start(out[bass.ds(i * (SUP * P), SUP * P), :].rearrange("(j p) n -> p j n", p=P),
                                  oacc[:, :, :]).then_inc(sem("out_st"), 16)
                else:
                    act.dma_start(out[(TILES - 1) * P:NODES, :], oacc[0:LAST, 0, :]).then_inc(sem("out_st"), 16)

            take_turned(0, SUP)
            router_exp(0, SUP)
            with act.Fori(0, SUPERS - 1) as i:
                feed(i, SUP, i + 1, SUP)
            feed(SUPERS - 1, SUP, SUPERS, 1)
            feed(SUPERS, 1, None, 0)

        @block.vector
        def _(dve):
            def tt(o, a, b, op):
                return dve.tensor_tensor(o, a, b, op)

            def rsqrt(link, var, eps, n=P, shape=None):
                w = var.shape[-1]
                v, y, t, u, q = (*(nrw[0:n, k, 0:w] for k in range(4)), nri[0:n, 0:w])
                if len(var.shape) == 3:
                    v, y, t, u = (nrw[0:n, k, 0:var.shape[1] * w].rearrange("p (l n) -> p l n", n=w) for k in range(4))
                    q = nri[0:n, 0:var.shape[1] * w].rearrange("p (l n) -> p l n", n=w)
                link(dve.tensor_scalar(v, var, eps, None, ALU.add))
                link(dve.tensor_scalar(q, v.bitcast(I32), 1, None, ALU.logical_shift_right))
                link(dve.tensor_scalar(y.bitcast(I32), q, -1.0, float(RSQRT_SEED), ALU.mult, ALU.add))
                for _ in range(NEWTON):
                    if w == 1:
                        link(dve.scalar_tensor_tensor(t, y, v, y, ALU.mult, ALU.mult))
                    else:
                        link(tt(t, y, y, ALU.mult))
                        link(tt(t, t, v, ALU.mult))
                    link(dve.tensor_scalar(u, t, -0.5, 1.5, ALU.mult, ALU.add))
                    link(tt(y, y, u, ALU.mult))
                return y

            start_ahead(dve, "dve")
            dve.memset(ident[:, :], 0.0).then_inc(sem("dve_const"), 1)
            dve.memset(chk_b[:, CHKN - 1:CHKN], FAR).then_inc(sem("dve_const"), 1)
            dve.memset(wblk[:, :], 0.0).then_inc(sem("dve_const"), 1)
            dve.memset(padc[:, :], 0).then_inc(sem("dve_const"), 1)
            dve.wait_ge(sem("dve_const"), 4)
            dve.memset(padc[:, PADE:2 * PADE], FAR).then_inc(sem("dve_const"), 1)
            dve.memset(zrow[:, :], 0.0).then_inc(sem("dve_const"), 1)
            dve.memset(fdst[:, :], FAR).then_inc(sem("dve_const"), 1)
            dve.memset(rowmask[:, :], 1.0).then_inc(sem("dve_const"), 1)
            dve.memset(ones[:, :], 1.0).then_inc(sem("dve_const"), 1)
            dve.memset(kvmask[:, :], 0.0).then_inc(sem("dve_const"), 1)
            dve.memset(headmask[:, :], 0.0).then_inc(sem("dve_const"), 1)
            dve.wait_ge(sem("dve_const"), 11)
            for q in range(4):
                b = slice(HD * q, HD * (q + 1))
                dve.memset(kvmask[b, b], 1.0).then_inc(sem("dve_const"), 1)
                dve.memset(headmask[b, q:q + 1], 1.0).then_inc(sem("dve_const"), 1)

            link = Chain(dve, "dve_chain")
            dve.wait_ge(sem("chk_in"), 48)
            link(tt(chk_c, chk_a, chk_b, ALU.is_gt))
            dve.tensor_reduce(flagf[0:CHKP, :], chk_c, AX.X, ALU.max).then_inc(sem("chk_max"), 1)
            dve.wait_ge(sem("chk_sum"), 1)
            dve.tensor_scalar(flag[:, :], bank(2, 0, 1)[0:1, :], 0.0, None, ALU.is_gt).then_inc(sem("flag_ready"), 1)

            NORM = 2 * LT + 3 + 4 * NEWTON
            ln0 = link.n

            def normalise(h, tiles, count):
                for t in range(tiles):
                    link.put(dve.bn_stats(lns[:, t, :], lnx[:, h, t, :]))
                wait_apart(dve, "dve_chain", link.n)
                for t in range(tiles):
                    link.put(dve.bn_aggr(lnmv[:, t, :], lns[:, t, :]))
                link.need()
                y = rsqrt(link, lnmv[:, 0:tiles, 1], LN_EPS)
                for t in range(tiles):
                    dve.tensor_scalar(lnx[:, h, t, :], lnx[:, h, t, :], lnmv[:, t, 0:1], y[:, t:t + 1],
                                      ALU.subtract, ALU.mult).then_inc(sem(f"ln_n{h}"), 1)
                dve.wait_ge(sem(f"ln_n{h}"), count)

            with dve.Fori(0, LG) as i:
                link.n = ln0 + i * (2 * NORM)
                for h in range(2):
                    dve.wait_ge(sem(f"ln_ld{h}"), 16 * (i + 1))
                    normalise(h, LT, LT * (i + 1))
            link.n = ln0 + LG * 2 * NORM
            dve.wait_ge(sem("ln_st0"), DLEAD + 16 * LG)
            dve.memset(lnx[:, 0, 0, :], 0.0).then_inc(sem("ln_zero"), 1)
            dve.wait_ge(sem("ln_ld0"), 16 * (LG + 1))
            normalise(0, 1, LT * LG + 1)

            dve.wait_ge(sem("flag_ready"), 1)
            unsorted = dve.value_load(flag[0:1, 0:1], min_val=0, max_val=1)
            with dve.If(unsorted > 0):
                real = EDGES - (P - 1) * CHUNKS
                dve.memset(s_dst[:, real:CHUNKS], FAR).then_inc(sem("s_fill"), 1)
                dve.memset(s_oth[:, :, real:CHUNKS], 0).then_inc(sem("s_fill"), 1)
                dve.memset(s_all, 1.0).then_inc(sem("s_const"), 1)
                dve.memset(s_low, 1.0).then_inc(sem("s_lowone"), 1)
                dve.memset(s_run, 0.0).then_inc(sem("s_const"), 1)
                dve.wait_ge(sem("s_in"), 128)
                dve.wait_ge(sem("s_const"), 4)
                slink = Chain(dve, "s_chain")
                slink(dve.tensor_scalar(s_rank.bitcast(I32), s_dst, 4, None, ALU.logical_shift_right))
                slink(dve.tensor_scalar(s_key, s_rank.bitcast(I32), float(SORTK - 1), None, ALU.min))

                def one_hot(i):
                    slink(dve.tensor_scalar(s_one, s_iota, s_key[:, bass.ds(i, 1)], None, ALU.is_equal))

                RANK = 6
                with dve.Fori(0, CHUNKS) as i:
                    slink.n = i * RANK + 2
                    one_hot(i)
                    dve.wait_ge(sem("s_mm"), i + 1)
                    slink(tt(s_tmp, bank(0, 0, SORTK), s_run, ALU.add))
                    slink(tt(s_tmp, s_tmp, s_one, ALU.mult))
                    slink(dve.tensor_reduce(s_col[:, 0:1], s_tmp, AX.X, ALU.add))
                    slink(dve.tensor_copy(s_rank[:, bass.ds(i, 1)], s_col[:, 0:1]))
                    slink(tt(s_run, s_run, bank(1, 0, SORTK), ALU.add))
                slink.n = CHUNKS * RANK + 2
                slink(dve.memset(s_start, 1.0))
                slink(dve.tensor_tensor_scan(s_tmp, s_start, s_run, 0.0, ALU.mult, ALU.add))
                slink(tt(s_start, s_tmp, s_run, ALU.subtract))
                PLACE = 8
                with dve.Fori(0, CHUNKS) as i:
                    slink.n = i * PLACE + CHUNKS * RANK + 5
                    one_hot(i)
                    slink(tt(s_tmp, s_start, s_one, ALU.mult))
                    slink(dve.tensor_reduce(s_col[:, 0:1], s_tmp, AX.X, ALU.add))
                    dve.wait_ge(sem("s_scat"), DLEAD + 16 * i)
                    slink(tt(s_idx, s_col[:, 0:1], s_rank[:, bass.ds(i, 1)], ALU.add))
                    slink(dve.tensor_copy(s_rec[:, 0:1], s_oth[:, 0, bass.ds(i, 1)]))
                    slink(dve.tensor_copy(s_rec[:, 1:2], s_dst[:, bass.ds(i, 1)]))
                    slink(dve.tensor_copy(s_rec[:, 2:3], s_oth[:, 1, bass.ds(i, 1)]))
                    slink(dve.tensor_copy(s_rec[:, 3:4].bitcast(F32), s_oth[:, 2, bass.ds(i, 1)].bitcast(F32)))
                    dve.nop().then_inc(sem("s_recs"), 1)
                for j in range(CB):
                    n = P if j < CB - 1 else CREST
                    dve.wait_ge(sem("s_rin"), 16 * (j + 1))
                    frm = s_blk[0:n, 0, :].rearrange("p (e f) -> p f e", f=4)
                    to = s_blk[0:n, 1, :].rearrange("p (f e) -> p f e", f=4)
                    dve.tensor_copy(to[:, 0:3, :], frm[:, 0:3, :]).then_inc(sem("s_turn"), 1)
                    dve.tensor_copy(to[:, 3, :].bitcast(F32), frm[:, 3, :].bitcast(F32)).then_inc(sem("s_turn"), 1)

            dve.wait_ge(sem("fdst_in"), 32)
            dve.wait_ge(sem("pool_const"), 10)
            link(dve.tensor_scalar(fgrp[:, :], fdst[:, :], 4, None, ALU.logical_shift_right))
            link(tt(tcol[:, :], fgrp[:, :], chunk_no[:, :], ALU.add))
            link(dve.memset(tcol[0:1, 0:1], float(4 * SPAD)))
            for j in range(CB):
                if j >= 2:
                    dve.wait_ge(sem("spread"), j - 1)
                dve.tensor_scalar(diag[:, j % 2, :], ident[:, :], tcol[:, j:j + 1], None, ALU.mult
                                  ).then_inc(sem("diag_ready"), 1)
            dve.wait_ge(sem("spread"), CB)
            for j in range(SB):
                dve.tensor_scalar(junk, PS[:, 4 * 512:4 * 512 + CB * P], step_no[:, j:j + 1], 0.0,
                                  ALU.is_le, ALU.add, accum_out=cstep[:, j:j + 1]).then_inc(sem("cstep_ready"), 1)
                dve.wait_ge(sem("cstep_ready"), j + 1)
            link(dve.memset(cint[:, SB:SB + 4], 0))
            link(dve.memset(gbase[:, 1, SB:SB + 4], 0.0))
            link(dve.tensor_copy(cint[:, 0:SB], cstep[:, :]))
            link(dve.scalar_tensor_tensor(gbase[:, 0, 0:SB], cstep[:, :], -1.0, step_no[:, :], ALU.mult, ALU.add))
            link(dve.tensor_scalar(gbase[:, 1, 0:SB], gbase[:, 0, 0:SB], float(GN), None, ALU.mult))

            dve.wait_ge(sem("bn_in"), 160)
            b_, g_, be_, m_, v_ = (bnrow[:, n:n + 6:5, :] for n in range(5))
            y = rsqrt(link, v_, BN_EPS, 2 * EXPERTS)
            link(tt(bnt[:, 0:4:2, :], g_, y, ALU.mult))
            link(tt(bnd, b_, m_, ALU.subtract))
            link(tt(bnd, bnd, bnt[:, 0:4:2, :], ALU.mult))
            tt(bnt[:, 1:4:2, :], bnd, be_, ALU.add).then_inc(sem("bn_folded"), 1)
            dve.wait_ge(sem("crow_in"), 16)
            link(dve.memset(crow[:, 0:1], 0.0))
            dve.tensor_tensor(keep, crow[:, 1:SPAD + 1], crow[:, 0:SPAD], ALU.subtract).then_inc(sem("tables_ready"), 1)
            dve.wait_ge(sem("tables_ready"), 1)
            dve.scalar_tensor_tensor(grow, crow[0:1, 1:SPAD + 1], -1.0, grow, ALU.mult, ALU.add
                                     ).then_inc(sem("tables_ready"), 1)

            def column(n, u):
                dve.tensor_copy(colg[:, u:u + 1], gbase[:, 1, bass.ds(n, 1)]).then_inc(sem("colg_ready"), 1)
                dve.tensor_copy(colc[:, u:u + 1], cint[:, bass.ds(n, 1)]).then_inc(sem("col_ready"), 1)

            for u in range(4):
                column(u, u)
            with dve.Fori(0, SB // 4) as i:
                for u in range(4):
                    dve.wait_ge(sem(f"irec_in{u}"), 16 * (i + 1))
                    dve.wait_ge(sem(f"rels_out{u}"), DLEAD + 16 * i)
                    dve.wait_ge(sem("fld_tp"), LEAD + 4 * i + (u - 1 if u else 0))
                    dve.wait_ge(sem("colg_ready"), 4 * i + u + 1)
                    dve.tensor_copy(ifld[:, u, 0, :], irec[:, u, 0:P]).then_inc(sem("fld_ready"), 1)
                    dve.tensor_scalar(ifld[:, u, 1, :], irec[:, u, P:2 * P], colg[:, u:u + 1], None, ALU.subtract
                                      ).then_inc(sem("fld_ready"), 1)
                    dve.tensor_copy(ifld[:, u, 2, :], irec[:, u, 2 * P:3 * P]).then_inc(sem("fld_type"), 1)
                    if u:
                        dve.wait_ge(sem("fld_tp"), LEAD + 4 * i + u)
                        dve.wait_ge(sem("fld_type"), 4 * i + u)
                        column(4 * i + 4 + u - 1, u - 1)
                dve.wait_ge(sem("fld_tp"), LEAD + 4 * i + 4)
                dve.wait_ge(sem("fld_type"), 4 * i + 4)
                column(4 * i + 7, 3)

            def rel_hot(it):
                dve.wait_ge(sem("types_in"), 64 * (it + 1))
                dve.wait_ge(sem("coef_mm"), LEAD + it)
                dve.tensor_scalar(relhot, relb, relcol[:, 0:1], None, ALU.is_equal).then_inc(sem("relhot_ready"), 1)

            def dst_hot(it):
                dve.wait_ge(sem("sel_ready"), LEAD + NB * it)
                dve.tensor_tensor(hot, table[:, 1, bass.ds(it * UN, UN)].unsqueeze(2).to_broadcast([P, UN, GN]),
                                  iota16[:, :].unsqueeze(1).to_broadcast([P, UN, GN]), ALU.is_equal
                                  ).then_inc(sem("hot_ready"), 1)

            def coefs(it):
                dve.wait_ge(sem("coef_mm"), LEAD + it + 1)
                dve.tensor_tensor(coef, bank(6, 0, UN * BASES).rearrange("p (s b) -> p s b", b=BASES),
                                  table[:, 2, bass.ds(it * UN, UN)].unsqueeze(2).to_broadcast([P, UN, BASES]), ALU.mult
                                  ).then_inc(sem("coef_ready"), 1)

            def select(it, q, free):
                dve.wait_ge(sem("hot_ready"), it + 1)
                dve.wait_ge(sem("coef_ready"), LEAD + it + 1)
                dve.wait_ge(sem("mm_done"), free)
                s = slice(q * BATCH, (q + 1) * BATCH)
                dve.tensor_tensor(selm[:, q % 2, :, :, :],
                                  hot[:, s, :].unsqueeze(3).to_broadcast([P, BATCH, GN, BASES]),
                                  coef[:, s, :].unsqueeze(2).to_broadcast([P, BATCH, GN, BASES]), ALU.mult
                                  ).then_inc(sem("sel_ready"), 1)

            def indices(it, h):
                dve.tensor_copy(idxc[:, h * RING:(h + 1) * RING], table[:, 0, bass.ds(it * UN + h * RING, RING)]
                                ).then_inc(sem("idx_ready"), 1)

            def keeps(it):
                dve.tensor_copy(keepc, keep[:, bass.ds(it * UN, UN)]).then_inc(sem("keepc_ready"), 1)

            dve.wait_ge(sem("table_cp"), LEAD + SB)
            dve.wait_ge(sem("tables_ready"), 2)
            for u in range(4):
                dve.wait_ge(sem(f"rels_out{u}"), DLEAD + 16 * (SB // 4))
            rel_hot(0)
            dst_hot(0)
            coefs(0)
            dve.wait_ge(sem("mm_credit"), 1)
            select(0, 0, RING)
            indices(0, 0)
            keeps(0)
            dve.memset(acc[:, RING - 1, :], 0.0).then_inc(sem("acc_zero"), 1)
            dve.wait_ge(sem("acc_zero"), 1)
            dve.sem_inc(sem("acc_done"), SLOTS)

            def steps(it, extra):
                for k in range(UN):
                    s = it * UN + k
                    if k == 0:
                        select(it, 1, it * UN + RING)
                        indices(it, 1)
                        dve.wait_ge(sem("keepc_ready"), it + 1)
                    if k == BATCH:
                        select(it, 2, it * UN + BATCH + RING)
                    if k == 7:
                        rel_hot(it + 1)
                    if k == 2 * BATCH:
                        select(it, 3, it * UN + 2 * BATCH + RING)
                        indices(it + 1, 0)
                    if k == 12:
                        dst_hot(it + 1)
                    if k == 13:
                        coefs(it + 1)
                    if k == 3 * BATCH:
                        select(it + 1, 0, it * UN + 3 * BATCH + RING)
                    dve.wait_ge(sem("mm_done"), s + 1 + RING)
                    dve.wait_ge(sem("acc_done"), s + SLOTS)
                    dve.wait_ge(sem(f"flush{k % RING}"), DLEAD + 32 * it + 16 * (k // RING))
                    a = (k % SLOTS) * 512
                    dve.scalar_tensor_tensor(acc[:, k % RING, :], acc[:, (k - 1) % RING, :], keepc[:, k:k + 1],
                                             PS[:, a:a + C], ALU.mult, ALU.add).then_inc(sem("acc_done"), 1)
                    if k in extra:
                        extra[k]()
                dve.wait_ge(sem("acc_done"), (it + 1) * UN + SLOTS)
                keeps(it + 1)

            with dve.Fori(0, TILES) as i:
                def m1_k():
                    dve.wait_ge(sem("m1_parts"), 2 * i + 2)
                    dve.wait_ge(sem("m1_acc"), LEAD + i)
                    dve.scalar_tensor_tensor(ksb, ek, 1.0, rk, ALU.min, ALU.add).then_inc(sem("m1_k"), 1)

                def m1_q():
                    dve.wait_ge(sem("m1_qparts"), LEAD + 2 * i + 2)
                    dve.wait_ge(sem("query_out"), DLEAD + 16 * i)
                    dve.scalar_tensor_tensor(qt[:, :, :].rearrange("p k n -> p (k n)"), eq, 1.0, rq, ALU.min, ALU.add
                                             ).then_inc(sem("m1_q"), 1)

                def m1_plus():
                    dve.wait_ge(sem("w_in"), 16 * 17)
                    dve.wait_ge(sem("xt_in"), 16 * (i + 1))
                    dve.wait_ge(sem("shift_out"), DLEAD + 16 * i)
                    tt(shifted, xt, lnw[:, 1, :], ALU.add).then_inc(sem("m1_plus"), 1)
                steps(i, {3: m1_plus, 8: m1_k, 9: m1_q})

            dve.wait_ge(sem("m1_acc"), LEAD + TILES)
            for h in range(KH):
                a = h * (P + 1)
                tt(kvb[:, h, 0:P], bank(7, a, a + P), kvmask[:, :], ALU.mult).then_inc(sem("kvb_ready"), 1)
                dve.tensor_scalar(kvb[:, h, P:P + 4], headmask[:, :], bank(7, a + P, a + P + 1), None, ALU.mult
                                  ).then_inc(sem("kvb_ready"), 1)

            MIXED = 2 + 2 + 5 + 1
            mix0 = link.n
            num = bank(6, QN, QN + 2 * (P + 4)).rearrange("p (k n) -> p k n", k=KH)

            def stats(link, n, ps):
                link.put(dve.bn_stats(lst[:, n, :], ps))

            def aggregate(link, n):
                dve.bn_aggr(lmv[:, n, :], lst[:, n, :]).then_inc(sem("ln_mv"), 1)

            def var_eps(i, a, n):
                dve.wait_ge(sem("ln_mv"), n)
                dve.tensor_scalar(lnr[:, 0, a:2], lmv[:, a:2, 1], LN_EPS, None, ALU.add).then_inc(sem("ln_var"), 1)

            def inverse(i, a, n):
                v, y, t, u, w = lnr[:, 0, a:2], lnr[:, 2, a:2], lnr[:, 3, a:2], lnu[:, 0, a:2], lnu[:, 1, a:2]
                if n == 0:
                    dve.wait_ge(sem("ln_root"), i + 1)
                    link.put(dve.reciprocal(y, lnr[:, 1, a:2]))
                    return
                link.need()
                if n == 1:
                    link.put(tt(t, y, y, ALU.mult))
                elif n == 2:
                    link.put(tt(t, t, v, ALU.mult))
                elif n == 3:
                    link.put(dve.tensor_scalar(u, t, -0.5, 1.5, ALU.mult, ALU.add))
                elif n == 4:
                    link.put(tt(w, y, u, ALU.mult))

            def m2_sum(i):
                dve.wait_ge(sem("m2_w1"), LEAD + i + 1)
                dve.wait_ge(sem("hidden_in"), 16 * (i + 1))
                dve.wait_ge(sem("m2_h"), LEAD + i)
                tt(hsum[:, :, :].rearrange("p k n -> p (k n)"), bank(7), hpart[:, :, :].rearrange("p k n -> p (k n)"),
                   ALU.add).then_inc(sem("m2_sum"), 1)

            def m2_base(i):
                link.put(dve.scalar_tensor_tensor(mo2, bank(7, 0, C), lmv[:, 1, 0:1], lnw[:, 0, :], ALU.subtract,
                                              ALU.mult))

            def m2_base2(i):
                link.need()
                dve.wait_ge(sem("shift_in"), 16 * (i + 1))
                dve.wait_ge(sem("base_out"), DLEAD + 16 * i)
                dve.scalar_tensor_tensor(mo, mo2, lnu[:, 1, 1:2], shifted, ALU.mult, ALU.add
                                         ).then_inc(sem("m2_base"), 1)

            with dve.Fori(0, TILES) as i:
                def m2_z():
                    dve.wait_ge(sem("m2_msg"), LEAD + i + 1)
                    link.n = mix0 + i * MIXED
                    link.put(dve.tensor_scalar(zt[:, :].rearrange("p (k n) -> p k n", k=KH), num[:, :, P:P + 4], ATT_EPS,
                                               None, ALU.add))

                def m2_zi():
                    link.need()
                    link.put(dve.reciprocal(zi[:, :], zt[:, :]))

                def m2_m():
                    link.need()
                    dve.wait_ge(sem("m2_tm"), LEAD + i)
                    for k in range(KH):
                        dve.scalar_tensor_tensor(
                            msb[:, k * P:(k + 1) * P].rearrange("p (h v) -> p h v", v=HD),
                            num[:, k, 0:P].rearrange("p (h v) -> p h v", v=HD), float(NODES),
                            zi[:, 4 * k:4 * k + 4].unsqueeze(2).to_broadcast([P, 4, HD]), ALU.mult, ALU.mult
                        ).then_inc(sem("m2_mm"), 1)

                def m2_stats1():
                    dve.wait_ge(sem("m2_w2"), LEAD + i + 1)
                    stats(link, 1, bank(7, 0, C))

                def m2_stats0():
                    dve.wait_ge(sem("m2_wm"), LEAD + i + 1)
                    stats(link, 0, bank(5, 0, C))

                def m2_aggr():
                    wait_apart(dve, "dve_chain", link.n)
                    aggregate(link, 1)
                    aggregate(link, 0)

                def m2_shift1():
                    link.need()
                    dve.scalar_tensor_tensor(shift1[:, :], lmv[:, 0, 0:1], -1.0, lnu[:, 1, 0:1], ALU.mult, ALU.mult
                                             ).then_inc(sem("ln_scale"), 1)

                steps(i + TILES, {1: m2_z, 2: m2_zi, 3: m2_m, 6: lambda: m2_sum(i), 9: m2_stats0, 11: m2_stats1,
                                  12: m2_aggr, 13: lambda: var_eps(i, 0, 2 * i + 2),
                                  14: lambda: inverse(i, 0, 0), 15: lambda: inverse(i, 0, 1),
                                  16: lambda: (inverse(i, 0, 2), m2_base(i)), 17: lambda: inverse(i, 0, 3),
                                  18: lambda: (inverse(i, 0, 4), m2_shift1()), 19: lambda: m2_base2(i)})
            link.n = mix0 + TILES * MIXED
            m2_sum(TILES)
            dve.wait_ge(sem("m2_w2"), LEAD + TILES + 1)
            stats(link, 1, bank(7, 0, C))
            link.need()
            aggregate(link, 1)
            var_eps(TILES, 1, 2 * TILES + 1)
            for n in range(5):
                inverse(TILES, 1, n)
            m2_base(TILES)
            m2_base2(TILES)
            dve.nop().then_inc(sem("main_over"), 1)

            ff0 = link.n
            dve.wait_ge(sem("main_over"), 4)
            for r in range(RING):
                dve.wait_ge(sem(f"flush{r}"), DLEAD + 16 * ITERS * UN // RING)
            FNORM = 2 * SUP + 3 + 4 * NEWTON + 4

            def sum_up(i, j, tiles):
                if j == 0:
                    if tiles < SUP:
                        dve.wait_ge(sem("b_x"), LEAD + SUPERS * SUP)
                        dve.memset(x_in[:, 0, :], 0.0).then_inc(sem("x_zero"), 1)
                    link.n = ff0 + i * FNORM
                    dve.wait_ge(sem("bx_in"), 32 * (i + 1))
                dve.wait_ge(sem("b_mm"), LEAD + i * SUP + j + 1)
                dve.scalar_tensor_tensor(xr[:, j, :], bank(6 + j % 2, 0, C), 0.0, base_in[:, j, :], ALU.max, ALU.add
                                         ).then_inc(sem("b_r"), 1)
                dve.wait_ge(sem("b_r"), LEAD + i * SUP + j + 1)
                tt(x1[:, j, :], xr[:, j, :], x_in[:, j, :], ALU.add).then_inc(sem("b_x"), 1)
                dve.wait_ge(sem("b_x"), LEAD + i * SUP + j + 1)
                link(dve.bn_stats(bst[:, j, :], x1[:, j, :]), apart=True)
                link(dve.bn_aggr(bmv[:, j, :], bst[:, j, :]))

            def norm(i, tiles):
                y = rsqrt(link, bmv[:, 0:tiles, 1], LN_EPS)
                dve.wait_ge(sem("b_tp"), LEAD + i * SUP)
                for j in range(tiles):
                    dve.tensor_scalar(x1n[:, j, :], x1[:, j, :], bmv[:, j, 0:1], y[:, j:j + 1], ALU.subtract, ALU.mult
                                      ).then_inc(sem("b_n"), 1)

            def per(t, tiles):
                return t[:, 0:tiles * EXPERTS].rearrange("p (j e) -> p j e", e=EXPERTS)

            def wide(t, tiles):
                return t[:, 0:tiles].unsqueeze(2).to_broadcast([P, tiles, EXPERTS])

            def router(i, tiles):
                dve.wait_ge(sem("r_lg"), i + 1)
                link(tt(per(lg, tiles), bank(7, 0, tiles * EXPERTS).rearrange("p (j e) -> p j e", e=EXPERTS),
                        br_s[:, :].unsqueeze(1).to_broadcast([P, tiles, EXPERTS]), ALU.add))
                link(dve.tensor_reduce(rmx[:, 0:tiles], per(lg, tiles), AX.X, ALU.max))
                tt(per(lg, tiles), per(lg, tiles), wide(rmx, tiles), ALU.subtract).then_inc(sem("r_sub"), 1)
                dve.wait_ge(sem("r_exp"), i + 1)
                link(dve.tensor_reduce(rsm[:, 0:tiles], per(ex, tiles), AX.X, ALU.add))
                link(dve.reciprocal(rin[:, 0:tiles], rsm[:, 0:tiles]))

            def feed(i, tiles, nxt, ntiles):
                dve.wait_ge(sem("o_upd"), LEAD + SUP * (EXPERTS + 1) * i)
                tt(per(rw, tiles), per(ex, tiles), wide(rin, tiles), ALU.mult).then_inc(sem("r_w"), 1)
                dve.wait_ge(sem("r_w"), i + 1)
                o0 = SUP * (EXPERTS + 1) * i
                dve.wait_ge(sem("out_st"), DLEAD + 16 * i)
                dve.wait_ge(sem("f_bo"), i + 1)
                for j in range(tiles):
                    tt(oacc[:, j, :], bank(4 + j // 2, (j % 2) * C, (j % 2) * C + C), x1[:, j, :], ALU.add
                       ).then_inc(sem("o_upd"), 1)
                for e in range(EXPERTS):
                    if e == EXPERTS - 1 and ntiles:
                        router(nxt, ntiles)
                    for j in range(tiles):
                        dve.wait_ge(sem("f_l3"), LEAD + SUP * EXPERTS * i + tiles * e + min(j // 2 * 2 + 2, tiles))
                        dve.wait_ge(sem("o_upd"), LEAD + o0 + tiles * e + j + 1)
                        dve.scalar_tensor_tensor(oacc[:, j, :], bank(4 + j // 2, (j % 2) * C, (j % 2) * C + C),
                                                 rw[:, EXPERTS * j + e:EXPERTS * j + e + 1], oacc[:, j, :],
                                                 ALU.mult, ALU.add).then_inc(sem("o_upd"), 1)
                    if e < ntiles:
                        sum_up(nxt, e, ntiles)
                    if e == SUP and ntiles:
                        norm(nxt, ntiles)

            for j in range(SUP):
                sum_up(0, j, SUP)
            norm(0, SUP)
            router(0, SUP)

            with dve.Fori(0, SUPERS - 1) as i:
                feed(i, SUP, i + 1, SUP)
            feed(SUPERS - 1, SUP, SUPERS, 1)
            feed(SUPERS, 1, None, 0)

        @block.tensor
        def _(pe):
            def mm(o, a, b, start=True, stop=True):
                return pe.matmul(o, a, b, start=start, stop=stop)

            start_ahead(pe, "pe")
            pe.wait_ge(sem("dve_const"), 19)
            pe.wait_ge(sem("pool_const"), 10)
            pe.wait_ge(sem("chk_max"), 1)
            mm(bank(2, 0, 1)[0:1, :], flagf[0:CHKP, :], ones[0:CHKP, 0:1]).then_inc(sem("chk_sum"), 1)

            pe.wait_ge(sem("flag_ready"), 1)
            unsorted = pe.value_load(flag[0:1, 0:1], min_val=0, max_val=1)
            with pe.If(unsorted > 0):
                pe.wait_ge(sem("s_const"), 4)
                with pe.Fori(0, CHUNKS) as i:
                    pe.wait_ge(sem("s_chain"), i * 6 + 3)
                    mm(bank(0, 0, SORTK), s_low, s_one)
                    mm(bank(1, 0, SORTK), s_all, s_one).then_inc(sem("s_mm"), 1)

            for j in range(CB):
                pe.wait_ge(sem("diag_ready"), j + 1)
                mm(PS[:, 4 * 512 + j * P:4 * 512 + (j + 1) * P], ones[:, :], diag[:, j % 2, :]
                   ).then_inc(sem("spread"), 1)
            pe.wait_ge(sem("bn_folded"), 1)
            for a in range(4):
                last = pe.transpose(bank(3, 2 * EXPERTS * a, 2 * EXPERTS * (a + 1)), bnt[:, a, :],
                                    ident[0:2 * EXPERTS, 0:2 * EXPERTS])
            last.then_inc(sem("bn_tp"), 1)
            with pe.Fori(0, SB // 4) as i:
                for u in range(4):
                    pe.wait_ge(sem("fld_ready"), 2 * (4 * i + u + 1))
                    pe.wait_ge(sem("table_cp"), LEAD + 4 * i + (u - 1 if u >= 2 else 0))
                    b = bank(u % 2)
                    pe.transpose(b[:, 0:P], ifld[:, u, 0, :], ident[:, :])
                    pe.transpose(b[:, P:2 * P], ifld[:, u, 1, :], ident[:, :])
                    pe.transpose(b[:, 2 * P:3 * P], irec[:, u, 3 * P:4 * P].bitcast(F32), ident[:, :]
                                 ).then_inc(sem("fld_tp"), 1)

            def coef_mm(it):
                pe.wait_ge(sem("relhot_ready"), it + 1)
                pe.wait_ge(sem("coef_ready"), LEAD + it)
                for j in range(BATCH):
                    last = mm(bank(6, 4 * BASES * j, 4 * BASES * (j + 1)), relhot[:, j, :], wblk[:, :])
                last.then_inc(sem("coef_mm"), 1)

            pe.wait_ge(sem("w_in"), 16 * 17)
            pe.wait_ge(sem("bnc_ready"), 1)
            pe.wait_ge(sem("table_cp"), LEAD + SB)
            mm(bank(7, 0, KH * (P + 1)), zrow[:, 0:P], zrow[:, :])
            coef_mm(0)
            pe.sem_inc(sem("mm_done"), RING)
            pe.sem_inc(sem("mm_credit"), 1)

            def steps(it, extra):
                for k in range(UN):
                    s = it * UN + k
                    if k % BATCH == 0:
                        pe.wait_ge(sem("sel_ready"), LEAD + NB * it + k // BATCH + 1)
                    if k == 9:
                        coef_mm(it + 1)
                    pe.wait_ge(sem(f"row_in{k % RING}"), 32 * it + 16 * (k // RING) + 16)
                    pe.wait_ge(sem("acc_done"), s + 1)
                    a = (k % SLOTS) * 512
                    sel = selm[:, (k // BATCH) % 2, k % BATCH, :, :].rearrange("p n b -> p (n b)")
                    for h in range(KH):
                        last = mm(PS[:, a + h * P:a + (h + 1) * P], ring[:, k % RING, h * P:(h + 1) * P], sel)
                    last.then_inc(sem("mm_done"), 1)
                    if k in extra:
                        extra[k]()

            def turn(o, frm, name):
                for h in range(KH):
                    last = pe.transpose(o[:, h * P:(h + 1) * P], frm[:, h * P:(h + 1) * P], ident[:, :])
                last.then_inc(sem(name), 1)

            with pe.Fori(0, TILES) as i:
                def m1_turn():
                    pe.wait_ge(sem("xt_in"), 16 * (i + 1))
                    pe.wait_ge(sem("m1_xt"), LEAD + i)
                    pe.wait_ge(sem("m1_qparts"), LEAD + 2 * i)
                    turn(bank(4), xt, "m1_tp")

                def m1_kv():
                    pe.wait_ge(sem("m1_xt"), LEAD + i + 1)
                    pe.wait_ge(sem("m1_v"), LEAD + 2 * i)
                    pe.wait_ge(sem("m1_hid"), LEAD + i)
                    for h in range(KH):
                        last = mm(bank(5), xnt[:, h, :], wkv_s[:, h, :], h == 0, h == KH - 1)
                    last.then_inc(sem("m1_kv"), 1)

                def m1_query():
                    for o in range(KH):
                        for h in range(KH):
                            last = mm(bank(4, C + o * P, C + (o + 1) * P), wq_s[:, h, o * P:(o + 1) * P], xnt[:, h, :],
                                      h == 0, h == KH - 1)
                    last.then_inc(sem("m1_query"), 1)

                def m1_w1(o):
                    for h in range(KH):
                        last = mm(bank(5, o * P, (o + 1) * P), w1_s[:, h, o * P:(o + 1) * P], xnt[:, h, :],
                                  h == 0, h == KH - 1)
                    if o == 3:
                        last.then_inc(sem("m1_w1"), 1)

                def m1_acc():
                    pe.wait_ge(sem("m1_k"), LEAD + i + 1)
                    pe.wait_ge(sem("m1_v"), LEAD + 2 * i + 2)
                    for h in range(KH):
                        a = h * (P + 1)
                        last = pe.matmul(bank(7, a, a + P + 1), ksb[:, h * P:(h + 1) * P], vx[:, h, :],
                                         start=False, stop=False, skip_group_check=True)
                    last.then_inc(sem("m1_acc"), 1)
                steps(i, {1: m1_turn, 4: m1_kv, 5: m1_query, 10: m1_acc, 12: lambda: m1_w1(0), 13: lambda: m1_w1(1),
                          14: lambda: m1_w1(2), 15: lambda: m1_w1(3)})
            pe.wait_ge(sem("kvb_ready"), 2 * KH)
            pe.wait_ge(sem("m1_hid"), LEAD + TILES)
            pe.wait_ge(sem("m1_qparts"), LEAD + 2 * TILES)

            def m2_tn(i):
                pe.wait_ge(sem("m2_n1"), LEAD + i)
                turn(bank(4), n1, "m2_tn")

            def m2_w1(i, o):
                if o == 0:
                    pe.wait_ge(sem("m2_nt"), KH * (i + 1))
                    pe.wait_ge(sem("m2_base"), LEAD + i)
                for h in range(KH):
                    last = mm(bank(7, o * P, (o + 1) * P), w1_s[:, KH + h, o * P:(o + 1) * P], nt[:, h, :],
                              h == 0, h == KH - 1)
                if o == 3:
                    last.then_inc(sem("m2_w1"), 1)

            def m2_w2(i):
                pe.wait_ge(sem("m2_h"), LEAD + i + 1)
                for h in range(4):
                    last = mm(bank(7, 0, C), ht[:, h, :], w2_s[:, h, :], h == 0, h == 3)
                last.then_inc(sem("m2_w2"), 1)

            pe.wait_ge(sem("n1_fill"), 2)
            with pe.Fori(0, TILES) as i:
                def m2_msg():
                    pe.wait_ge(sem("query_in"), 16 * (i + 1))
                    pe.wait_ge(sem("coef_ready"), LEAD + TILES + 1 + i)
                    for h in range(KH):
                        last = mm(bank(6, QN + h * (P + 4), QN + (h + 1) * (P + 4)), qt[:, h, :], kvb[:, h, :])
                    last.then_inc(sem("m2_msg"), 1)

                def m2_tm():
                    pe.wait_ge(sem("m2_mm"), KH * (i + 1))
                    turn(bank(4), msb, "m2_tm")

                def m2_wm():
                    pe.wait_ge(sem("m2_mt"), i + 1)
                    for h in range(KH):
                        last = mm(bank(5, 0, C), mst[:, h, :], wm_s[:, h, :], h == 0, h == KH - 1)
                    last.then_inc(sem("m2_wm"), 1)

                def w1_first():
                    m2_w1(i, 0)
                    m2_w1(i, 1)

                def w1_second():
                    m2_w1(i, 2)
                    m2_w1(i, 3)
                steps(i + TILES, {0: m2_msg, 1: lambda: m2_tn(i), 4: w1_first, 5: w1_second, 7: m2_tm, 8: m2_wm,
                                  11: lambda: m2_w2(i)})
            m2_tn(TILES)
            for o in range(4):
                m2_w1(TILES, o)
            m2_w2(TILES)
            pe.nop().then_inc(sem("main_over"), 1)

            pe.wait_ge(sem("main_over"), 4)
            pe.wait_ge(sem("ffw_in"), 16 * 8)

            def combine(i, j):
                pe.wait_ge(sem(f"at_in{j}"), 32 * (i + 1))
                pe.wait_ge(sem("b_r"), LEAD + i * SUP + (j - 1 if j >= 2 else 0))
                agg = at_in[:, j, :, :, :].rearrange("p h g (n b) -> p h (g n) b", b=BASES)
                for b in range(BASES):
                    for h in range(KH):
                        last = mm(bank(6 + j % 2, 0, C), agg[:, h, :, b], bases_s[:, b, h, :],
                                  b == 0 and h == 0, b == BASES - 1 and h == KH - 1)
                last.then_inc(sem("b_mm"), 1)

            def turns(i, tiles):
                for j in range(tiles):
                    pe.wait_ge(sem("b_n"), i * SUP + j + 1)
                    pe.wait_ge(sem("b_xt"), LEAD + i * SUP + (j - 1 if j >= 2 else 0))
                    turn(bank(6 + j % 2, C, 2 * C), x1n[:, j, :], "b_tp")

            def logits(i, tiles):
                pe.wait_ge(sem("b_xt"), LEAD + i * SUP + tiles)
                for j in range(tiles):
                    for h in range(KH):
                        last = mm(bank(7, j * EXPERTS, (j + 1) * EXPERTS), x1t[:, h, j * P:(j + 1) * P], wr_s[:, h, :],
                                  h == 0, h == KH - 1)
                last.then_inc(sem("r_lg"), 1)

            def feed(i, tiles, nxt, ntiles):
                n = tiles * P
                o0 = SUP * (EXPERTS + 1) * i

                def layer(e, w, frm, b0, done):
                    for o in range(KH):
                        for h in range(KH):
                            last = mm(bank(b0 + o, 0, n), w[:, e, h, o * P:(o + 1) * P], frm[:, h, 0:n],
                                      h == 0, h == KH - 1)
                    last.then_inc(sem(done), 1)

                def first(e):
                    pe.wait_ge(sem("f_h1"), LEAD + KH * (EXPERTS * i + e))
                    layer(e, f1_s, x1t, 0, "f_l1")

                def second(e):
                    pe.wait_ge(sem("f_h1"), LEAD + KH * (EXPERTS * i + e + 1))
                    pe.wait_ge(sem("f_h2"), LEAD + KH * (EXPERTS * i + e))
                    layer(e, f2_s, h1, 2, "f_l2")

                def third(e):
                    pe.wait_ge(sem("f_h2"), LEAD + KH * (EXPERTS * i + e + 1))
                    pe.wait_ge(sem("o_upd"), LEAD + o0 + tiles * (e + 1))
                    for j in range(tiles):
                        for h in range(KH):
                            last = mm(bank(4 + j // 2, (j % 2) * C, (j % 2) * C + C), h2[:, h, j * P:(j + 1) * P],
                                      fo_s[:, e, h, :], h == 0, h == KH - 1)
                        last.then_inc(sem("f_l3"), 1)

                first(0)
                pe.wait_ge(sem("r_w"), i + 1)
                pe.wait_ge(sem("o_upd"), LEAD + o0)
                for j in range(tiles):
                    last = pe.transpose(bank(4, j * P, (j + 1) * P)[0:EXPERTS, :],
                                        rw[:, EXPERTS * j:EXPERTS * (j + 1)], ident[:, :])
                last.then_inc(sem("r_tp"), 1)
                pe.wait_ge(sem("r_wt"), i + 1)
                for j in range(tiles):
                    last = mm(bank(4 + j // 2, (j % 2) * C, (j % 2) * C + C), wt[:, j * P:(j + 1) * P], bo_s[:, :])
                last.then_inc(sem("f_bo"), 1)
                second(0)
                for e in range(1, EXPERTS):
                    first(e)
                    third(e - 1)
                    if e == EXPERTS - 1:
                        turns(nxt, ntiles)
                    second(e)
                    if e - 1 < ntiles:
                        combine(nxt, e - 1)
                if ntiles:
                    logits(nxt, ntiles)
                third(EXPERTS - 1)

            for j in range(SUP):
                combine(0, j)
            turns(0, SUP)
            logits(0, SUP)

            with pe.Fori(0, SUPERS - 1) as i:
                feed(i, SUP, i + 1, SUP)
            feed(SUPERS - 1, SUP, SUPERS, 1)
            feed(SUPERS, 1, None, 0)


_INS = ["x", "src", "dst", "edge_type_32", "edge_weight1", "L0_gnn_bases", "L0_gnn_w_comp", "L0_mix_Wq",
        "L0_mix_Wk", "L0_mix_Wv", "L0_mix_Wm", "L0_mix_W1", "L0_mix_W2", "L0_mix_g1", "L0_mix_b1", "L0_mix_g2",
        "L0_mix_b2", "L0_ffn_Wr", "L0_ffn_br", "L0_ffn_W1", "L0_ffn_b1", "L0_ffn_g1", "L0_ffn_be1", "L0_ffn_m1",
        "L0_ffn_v1", "L0_ffn_W2", "L0_ffn_b2", "L0_ffn_g2", "L0_ffn_be2", "L0_ffn_m2", "L0_ffn_v2", "L0_ffn_Wo",
        "L0_ffn_bo"]


def kernel(**inputs):
    import numpy as _np
    import concourse.bacc as _bacc
    from concourse import mybir as _mybir
    from concourse.bass_utils import run_bass_kernel_spmd as _run

    nc = _bacc.Bacc("TRN2", target_bir_lowering=False, num_devices=1)
    arrays, args = {}, []
    for name in _INS:
        a = _np.ascontiguousarray(inputs[name])
        arrays[f"in_{name}_dram"] = a
        args.append(nc.dram_tensor(f"in_{name}_dram", a.shape, _mybir.dt.from_np(a.dtype), kind="ExternalInput").ap())
    args.append(nc.dram_tensor("out_0_dram", (NODES, C), _mybir.dt.float32, kind="ExternalOutput").ap())
    gps_layer(nc, *args)
    r = _run(nc, [arrays], core_ids=[0])
    return r.results[0]["out_0_dram"]
```
